# Optimizing a Trainium2 kernel written in Bass

```python
import numpy as np
import jax
import jax.numpy as jnp

def _softmax(x, axis=-1):
    return jax.nn.softmax(x, axis=axis)

def _gelu(x):
    return jax.nn.gelu(x, approximate=True)

def _silu(x):
    return jax.nn.silu(x)

def _sigmoid(x):
    return jax.nn.sigmoid(x)

def _layernorm(x, axis=-1, eps=1e-05):
    m = jnp.mean(x, axis=axis, keepdims=True)
    v = jnp.var(x, axis=axis, keepdims=True)
    return (x - m) / jnp.sqrt(v + eps)

def _scatter_add(tgt, idx, src, axis=0):
    return tgt.at[idx].add(src)

def _segment_sum(src, seg, n):
    return jax.ops.segment_sum(src, seg, n)
kernel_name = 'mk_early_fusion_d1_tok_img1024_r4_56f3ea'

def setup_inputs(seed: int=0):
    np.random.seed(seed)
    _w = jnp.asarray

    def _rec_inputs():
        import jax
        import jax.numpy as jnp
        _rk = jax.random.key(seed)
        x = -0.000356955 + 1 * jax.random.normal(jax.random.fold_in(_rk, 1), (64, 3, 224, 224), jnp.float32)
        txt = -0.000394971 + 1.15376 * jax.random.normal(jax.random.fold_in(_rk, 2), (64, 77, 256), jnp.float32)
        return (x, txt)
    x, txt = _rec_inputs()

    def _L0_tok_setup():
        import jax, jax.numpy as jnp
        import numpy as np
        PATCH = 16
        H = W = 224
        C = 3
        NP_SIDE = H // PATCH
        NUM_PATCHES = NP_SIDE * NP_SIDE
        PATCH_DIM = C * PATCH * PATCH
        EMBED = 256
        key = jax.random.key(seed)
        k1, k2, k3, k4 = jax.random.split(key, 4)
        B = 128
        raw_pixels = jax.random.normal(k1, (B, C, H, W), dtype=jnp.float32)
        bound = 1.0 / np.sqrt(PATCH_DIM)
        W_embed = jax.random.uniform(k2, (PATCH_DIM, EMBED), minval=-bound, maxval=bound, dtype=jnp.float32)
        b_embed = jax.random.uniform(k3, (EMBED,), minval=-bound, maxval=bound, dtype=jnp.float32)
        pos_embed = jax.random.normal(k4, (1, NUM_PATCHES, EMBED), dtype=jnp.float32)
        return {'raw_pixels': raw_pixels, 'W_embed': W_embed, 'b_embed': b_embed, 'pos_embed': pos_embed}
    _L0_tok_all = _L0_tok_setup()
    _L0_tok_in = {k: v for k, v in _L0_tok_all.items() if k in ('W_embed', 'b_embed', 'pos_embed')}
    del _L0_tok_all

    def _L0_attn_setup():
        import jax, jax.numpy as jnp
        import numpy as np
        BETA = 1.0
        B, S, D = (4, 1024, 256)
        key = jax.random.key(seed)
        k_x, k_q, k_k, k_v = jax.random.split(key, 4)
        scale = 1.0 / np.sqrt(D)
        x = jax.random.normal(k_x, (B, S, D), dtype=jnp.float32)
        Wq = jax.random.uniform(k_q, (D, D), dtype=jnp.float32, minval=-scale, maxval=scale)
        Wk = jax.random.uniform(k_k, (D, D), dtype=jnp.float32, minval=-scale, maxval=scale)
        Wv = jax.random.uniform(k_v, (D, D), dtype=jnp.float32, minval=-scale, maxval=scale)
        return {'x': x, 'Wq': Wq, 'Wk': Wk, 'Wv': Wv}
    _L0_attn_all = _L0_attn_setup()
    _L0_attn_in = {k: v for k, v in _L0_attn_all.items() if k in ('Wq', 'Wk', 'Wv')}
    del _L0_attn_all

    def _L0_ffn_setup():
        import jax, jax.numpy as jnp
        import numpy as np
        DIM = 256
        HIDDEN = 768
        SCALE = 1.0 / 127.0

        def _dequant(w_int, dtype):
            return w_int.astype(dtype) * jnp.asarray(SCALE, dtype)
        key = jax.random.key(seed)
        k_x, k_g, k_u, k_d = jax.random.split(key, 4)
        x = jax.random.normal(k_x, (4, 512, DIM), dtype=jnp.float32)
        w_gate = jax.random.randint(k_g, (HIDDEN, DIM), -127, 128, dtype=jnp.int32)
        w_up = jax.random.randint(k_u, (HIDDEN, DIM), -127, 128, dtype=jnp.int32)
        w_down = jax.random.randint(k_d, (DIM, HIDDEN), -127, 128, dtype=jnp.int32)
        return {'x': x, 'w_gate': w_gate, 'w_up': w_up, 'w_down': w_down}
    _L0_ffn_all = _L0_ffn_setup()
    _L0_ffn_in = {k: v for k, v in _L0_ffn_all.items() if k in ('w_gate', 'w_up', 'w_down')}
    del _L0_ffn_all
    return {'x': x, 'txt': txt, 'L0_tok_W_embed': _L0_tok_in['W_embed'], 'L0_tok_b_embed': _L0_tok_in['b_embed'], 'L0_tok_pos_embed': _L0_tok_in['pos_embed'], 'L0_attn_Wq': _L0_attn_in['Wq'], 'L0_attn_Wk': _L0_attn_in['Wk'], 'L0_attn_Wv': _L0_attn_in['Wv'], 'L0_ffn_w_gate': _L0_ffn_in['w_gate'], 'L0_ffn_w_up': _L0_ffn_in['w_up'], 'L0_ffn_w_down': _L0_ffn_in['w_down']}

def reference(x, txt, L0_tok_W_embed, L0_tok_b_embed, L0_tok_pos_embed, L0_attn_Wq, L0_attn_Wk, L0_attn_Wv, L0_ffn_w_gate, L0_ffn_w_up, L0_ffn_w_down):
    import jax
    import jax.numpy as jnp

    def _L0_tok_ref(raw_pixels, W_embed, b_embed, pos_embed):
        import jax, jax.numpy as jnp
        import numpy as np
        PATCH = 16
        H = W = 224
        C = 3
        NP_SIDE = H // PATCH
        NUM_PATCHES = NP_SIDE * NP_SIDE
        PATCH_DIM = C * PATCH * PATCH
        EMBED = 256
        B = raw_pixels.shape[0]
        patches = raw_pixels.reshape(B, C, NP_SIDE, PATCH, NP_SIDE, PATCH)
        patches = patches.transpose(0, 2, 4, 1, 3, 5).reshape(B, NUM_PATCHES, PATCH_DIM)
        x = jnp.einsum('bnd,de->bne', patches, W_embed) + b_embed
        return x + pos_embed

    def _L0_attn_ref(x, Wq, Wk, Wv):
        import jax, jax.numpy as jnp
        import numpy as np
        BETA = 1.0
        B, S, D = (4, 1024, 256)
        q = jnp.einsum('bsd,ed->bse', x, Wq)
        k = jnp.einsum('bsd,ed->bse', x, Wk)
        v = jnp.einsum('bsd,ed->bse', x, Wv)
        scores = jnp.einsum('bqd,bkd->bqk', q, k)
        attn = jax.nn.softmax(BETA * scores, axis=-1)
        attended = jnp.einsum('bqk,bkd->bqd', attn, v)
        y = attended + x
        return y / jnp.linalg.norm(y, axis=-1, keepdims=True)

    def _L0_ffn_ref(x, w_gate, w_up, w_down):
        import jax, jax.numpy as jnp
        import numpy as np
        DIM = 256
        HIDDEN = 768
        SCALE = 1.0 / 127.0

        def _dequant(w_int, dtype):
            return w_int.astype(dtype) * jnp.asarray(SCALE, dtype)
        wg = _dequant(w_gate, x.dtype)
        wu = _dequant(w_up, x.dtype)
        wd = _dequant(w_down, x.dtype)
        gate = jnp.einsum('bsd,hd->bsh', x, wg)
        up = jnp.einsum('bsd,hd->bsh', x, wu)
        h = jax.nn.silu(gate) * up
        return jnp.einsum('bsh,dh->bsd', h, wd)
    h = _L0_tok_ref(x, L0_tok_W_embed, L0_tok_b_embed, L0_tok_pos_embed)
    h = jnp.concatenate([h, txt], axis=1)
    h = h + _L0_attn_ref(_layernorm(h, axis=-1), L0_attn_Wq, L0_attn_Wk, L0_attn_Wv)
    h = h + _L0_ffn_ref(_layernorm(h, axis=-1), L0_ffn_w_gate, L0_ffn_w_up, L0_ffn_w_down)
    return h

_drawn_inputs = setup_inputs


def setup_inputs(seed=0):
    import zlib

    import numpy as np

    out = dict(_drawn_inputs(seed))
    spreads = {}
    factors = {}
    for name, (base, spread) in spreads.items():
        noise = np.random.default_rng([zlib.crc32(name.encode()), seed]).standard_normal(out[name].shape)
        drawn = base * np.exp(spread * noise) if base else spread * noise
        out[name] = jnp.asarray(drawn.astype(out[name].dtype))
    for name, factor in factors.items():
        out[name] = (out[name] * factor).astype(out[name].dtype)
    return out
```

```python
from contextlib import ExitStack

import concourse.bass as bass
from concourse import mybir

F32 = mybir.dt.float32
F32R = mybir.dt.float32r
I32 = mybir.dt.int32
ALU = mybir.AluOpType
ACT = mybir.ActivationFunctionType
AX_X = mybir.AxisListType.X

P = 128
EPS = 1e-5
INT_SCALE = 1.0 / 127.0


def fusion_layer(nc, x, txt, w_embed, b_embed, pos_embed, wq, wk, wv, w_gate, w_up, w_down, out):
    images, channels, side, _ = x.shape
    text = txt.shape[1]
    dim = wq.shape[0]
    hidden = w_gate.shape[0]
    patches = pos_embed.shape[1]
    grid = side // 16
    patch = side // grid
    tokens = patches + text
    wide = tokens + 1
    half_rows = patches // 2
    ROWS = (half_rows, half_rows, text)
    FIRST = (0, half_rows, patches)
    T = len(ROWS)
    DC = dim // P
    HC = hidden // P
    STORES = 2 * 16
    PAIR = 2
    pairs = images // PAIR
    px_rows = PAIR * channels * grid
    px_cols = patch * side
    HALF = patch * patch // 2
    FILL = ((0, 5), (5, 10), (10, grid))
    FILLS = 2 * len(FILL)

    x_rows = x.rearrange("b c (g i) w -> (b c g) (i w)", i=patch)
    out_rows = out.rearrange("b s d -> (b s) d")
    txt_rows = txt.rearrange("b s d -> (b s) d")

    LAST, MIDDLE = True, False

    def bank_order(u, last):
        order = []
        if u == 1 and not last:
            order += ["fill0", "fill1"]
        order += ["probs0", "probs1", "probs2"]
        if u == 1 and not last:
            order += ["fill2", "fill3", "fill4", "fill5"]
        if not (u == 1 and last):
            order += ["x0", "x1"]
        return order + ["z0", "z1"]

    WEIGHT_GROUPS = 11
    BEFORE = WEIGHT_GROUPS + FILLS + DC
    PER_SLOT = (len(bank_order(0, MIDDLE)), len(bank_order(1, MIDDLE)))
    PER_BODY = sum(PER_SLOT)
    assert PER_BODY % 2 == 0

    def use_of(k, u, last, name):
        return k * PER_BODY + BEFORE + u * PER_SLOT[0] + bank_order(u, last).index(name)

    def bank_of(u, last, name):
        return (BEFORE + u * PER_SLOT[0] + bank_order(u, last).index(name)) % 2

    with ExitStack() as ctx:
        def sb(name, shape, dt=F32):
            return ctx.enter_context(nc.sbuf_tensor(name, shape, dt))

        def sem(name):
            return ctx.enter_context(nc.semaphore(name))

        def split(name, shape):
            return sb(name + "_hi", shape, F32R), sb(name + "_lo", shape, F32R)

        raw = sb("raw_pixels", [px_rows, px_cols])
        pix = sb("patch_pixels", [px_rows, grid, patch * patch])
        patT = split("patches_T", [P, 2, PAIR * channels * patches])
        we = split("w_embed", [P, 2 * channels, dim])
        wqk = split("w_qk", [P, DC, dim])
        wvT = split("wv_T", [P, DC, dim])
        wgT = split("w_gate_T", [P, DC, hidden])
        wuT = split("w_up_T", [P, DC, hidden])
        wdT = split("w_down_T", [P, HC, dim])
        wstage = [sb(f"w_stage{i}", [P, DC * hidden]) for i in range(2)]
        wint = sb("w_int", [P, DC * hidden], I32)
        pos = sb("pos_bias", [half_rows, 2, dim])
        bias = sb("bias_rows", [half_rows, dim])
        ident = sb("identity", [P, P])
        eps = sb("eps", [P, T])
        neg_half = sb("minus_half", [P, T])
        h = [sb(f"h{i}", [half_rows, T, dim]) for i in range(2)]
        xn = [sb(f"x_norm{i}", [half_rows, T, dim]) for i in range(2)]
        xT = split("x_T", [P, DC, wide])
        tT = split("xw_T", [P, DC, tokens])
        v = split("v", [half_rows, T, dim])
        probs = sb("probs", [half_rows, T, tokens])
        pT = split("probs_T", [half_rows, T, tokens])
        y = sb("y", [half_rows, T, dim])
        ysq = sb("y_squared", [half_rows, T, dim])
        h2 = [sb(f"h_mid{i}", [half_rows, T, dim]) for i in range(2)]
        z = sb("z_norm", [half_rows, T, dim])
        zT = split("z_T", [P, DC, wide])
        th = [sb(f"tanh{i}", [P, tokens]) for i in range(2)]
        ga = [sb(f"gated{i}", [P, tokens]) for i in range(2)]
        hid = [sb(f"hid{i}", [P, tokens]) for i in range(2)]
        hidT = split("hid_T", [P, HC, tokens])
        res = [sb(f"result{i}", [half_rows, T, dim]) for i in range(2)]
        stats = [sb(f"bn{i}", [half_rows, T, 6]) for i in range(2)]
        mv = [sb(f"mean_var{i}", [half_rows, T, 2]) for i in range(2)]
        var_eps = [sb(f"var_eps{i}", [half_rows, T]) for i in range(2)]
        rstd = [sb(f"rstd{i}", [half_rows, T]) for i in range(2)]
        nmax = sb("minus_max", [half_rows, T])
        den = sb("denominator", [half_rows, T])
        rden = sb("one_over_denominator", [half_rows, T])
        ssq = sb("y_square_sum", [half_rows, T])
        rnorm = sb("one_over_norm", [half_rows, T])

        def psum(name):
            return ctx.enter_context(nc.psum_tensor(name, [P, 512], F32))

        tp = [psum(f"transposing{i}") for i in range(2)]
        ab = [psum(f"attention{i}") for i in range(3)]
        fb = [psum(f"feed_forward{i}") for i in range(3)]

        consts_set = sem("consts_set")
        ident_set = sem("ident_set")
        w_loaded = [sem(f"w_loaded{i}") for i in range(7)]
        pos_loaded = sem("pos_loaded")
        w_float = sem("w_float")
        we_hi = sem("we_hi")
        we_split = sem("we_split")
        pos_set = sem("pos_set")
        px_loaded = sem("px_loaded")
        px_moved = sem("px_moved")
        text_loaded = [sem(f"text_loaded{i}") for i in range(2)]
        stored = [sem(f"stored{i}") for i in range(2)]
        transposed = sem("transposed")
        tp_hi = sem("transposed_hi")
        tp_split = sem("transposed_split")
        embedded = sem("embedded")
        h_added = sem("h_added")
        bn_done = [sem(f"bn_done{i}") for i in range(2)]
        mv_done = [sem(f"mv_done{i}") for i in range(2)]
        eps_done = [sem(f"eps_done{i}") for i in range(2)]
        rstd_done = [sem(f"rstd_done{i}") for i in range(2)]
        normed = [sem(f"normed{i}") for i in range(2)]
        projected = sem("projected")
        proj_hi = sem("proj_hi")
        proj_split = sem("proj_split")
        valued = sem("valued")
        v_hi = sem("v_hi")
        v_split = sem("v_split")
        scored = sem("scored")
        maxed = sem("maxed")
        exped = sem("exped")
        rden_done = sem("rden_done")
        attended = sem("attended")
        y_done = sem("y_done")
        squared = sem("squared")
        rnorm_done = sem("rnorm_done")
        h2_done = sem("h2_done")
        gate_done = sem("gate_done")
        up_done = sem("up_done")
        tanh_done = sem("tanh_done")
        gated = sem("gated")
        hid_done = sem("hid_done")
        hid_hi = sem("hid_hi")
        hid_split = sem("hid_split")
        downed = sem("downed")
        passed = {nc.vector: sem("dve_passed"), nc.gpsimd: sem("pool_passed")}
        final = sem("final")

        def need(eng, semaphore, value):
            if not (isinstance(value, int) and value <= 0):
                eng.wait_ge(semaphore, value)

        def need_apart(eng, semaphore, value):
            need(eng, semaphore, value)
            eng.sem_inc(passed[eng], 1)

        def flat(pair_of_parts):
            return [t[:].rearrange("p a b -> p (a b)") for t in pair_of_parts]

        block = ctx.enter_context(nc.Block())

        @block.sync
        def _(sp):
            sp.dma_start(raw[:, :], x_rows[0:px_rows, :]).then_inc(px_loaded, 16)
            for par in range(2):
                sp.sem_inc(stored[par], STORES)
            sp.dma_start(wstage[0][:, 0:DC * dim].rearrange("p (c d) -> p c d", c=DC),
                         wq.rearrange("(c p) d -> p c d", p=P)).then_inc(w_loaded[0], 16)
            sp.dma_start(wstage[0][:, DC * dim:2 * DC * dim].rearrange("p (c d) -> p c d", c=DC),
                         wk.rearrange("(c p) d -> p c d", p=P)).then_inc(w_loaded[1], 16)
            sp.dma_start(wstage[0][:, 2 * DC * dim:3 * DC * dim].rearrange("p (c d) -> p c d", c=DC),
                         wv.rearrange("(c p) d -> p c d", p=P)).then_inc(w_loaded[2], 16)
            sp.dma_start(wstage[1][:, :].rearrange("p (c d) -> p c d", d=dim),
                         w_embed.rearrange("(c p) d -> p c d", p=P)).then_inc(w_loaded[3], 16)
            sp.dma_start(pos[:, :, :], pos_embed.rearrange("o (t p) d -> p (o t) d", p=half_rows)
                         ).then_inc(pos_loaded, 16)
            sp.dma_start(bias[:, :], b_embed.rearrange("(o d) -> o d", o=1).to_broadcast([half_rows, dim])
                         ).then_inc(pos_loaded, 16)
            sp.dma_start(h[0][0:text, 2, :], txt_rows[0:text, :]).then_inc(text_loaded[0], 16)
            sp.dma_start(wint[:, :].rearrange("p (c d) -> p c d", d=dim),
                         w_gate.rearrange("(c p) d -> p c d", p=P)).then_inc(w_loaded[4], 16)
            sp.wait_ge(w_float, 1)
            sp.dma_start(wint[:, :].rearrange("p (c d) -> p c d", d=dim),
                         w_up.rearrange("(c p) d -> p c d", p=P)).then_inc(w_loaded[5], 16)
            sp.wait_ge(w_float, 2)
            sp.dma_start(wint[:, :].rearrange("p (c h) -> p c h", h=hidden),
                         w_down.rearrange("(c p) h -> p c h", p=P)).then_inc(w_loaded[6], 16)

            def store(m, par):
                need(sp, final, 3 * m + 3)
                sp.dma_start(out_rows[bass.ds(m * tokens, patches), :].rearrange("(t p) d -> p t d", p=half_rows),
                             res[par][:, 0:2, :]).then_inc(stored[par], 16)
                sp.dma_start(out_rows[bass.ds(m * tokens + patches, text), :],
                             res[par][0:text, 2, :]).then_inc(stored[par], 16)

            def body(k, first=False, last=False):
                for u in range(2):
                    n = 2 * k + u
                    if u == 0 and not last:
                        need(sp, px_moved, 2 * k + 2)
                        sp.dma_start(raw[:, :], x_rows[bass.ds((k + 1) * px_rows, px_rows), :]
                                     ).then_inc(px_loaded, 16)
                    if not (last and u == 1):
                        need(sp, h2_done, 3 * n)
                        sp.dma_start(h[1 - u][0:text, 2, :], txt_rows[bass.ds((n + 1) * text, text), :]
                                     ).then_inc(text_loaded[1 - u], 16)
                    if not (first and u == 0):
                        store(n - 1, 1 - u)

            body(0, first=True)
            with sp.Fori(1, pairs - 1) as k:
                body(k)
            body(pairs - 1, last=True)
            store(images - 1, 1)
            for par in range(2):
                sp.wait_ge(stored[par], STORES * (pairs + 1))

        @block.gpsimd
        def _(pool):
            nc.gpsimd.memset(ident[:, :], 0.0).then_inc(ident_set, 1)
            pool.wait_ge(ident_set, 1)
            nc.gpsimd.affine_select(out=ident[:, :], in_=ident[:, :], compare_op=ALU.not_equal, fill=1.0,
                                    base=0, pattern=[[-1, P]], channel_multiplier=1).then_inc(ident_set, 1)
            nc.gpsimd.memset(eps[:, :], EPS)
            nc.gpsimd.memset(neg_half[:, :], -0.5)
            for t in (xT[0], xT[1], zT[0], zT[1]):
                nc.gpsimd.memset(t[:, :, tokens:wide].bitcast(F32), 0.0)
            for t in (den, ssq, mv[0], mv[1]):
                last_set = nc.gpsimd.memset(t[:], 1.0)
            last_set.then_inc(consts_set, 1)

            def move_pixels(pair, transposes):
                for half in range(2):
                    if half == 0:
                        need_apart(pool, transposed, transposes)
                    need_apart(pool, px_loaded, 16 * pair + 16)
                    nc.gpsimd.tensor_copy(
                        pix[:, :, half * HALF:(half + 1) * HALF].rearrange("r g (i j) -> r g i j", j=patch),
                        raw[:, :].rearrange("r (i g j) -> r g i j", i=patch, j=patch)
                        [:, :, half * patch // 2:(half + 1) * patch // 2, :]).then_inc(px_moved, 1)

            def inverse_std(which, n):
                need(pool, mv_done[which], 3 * n + 3)
                nc.gpsimd.tensor_tensor(var_eps[which][:, :], mv[which][:, :, 1], eps[0:half_rows, :],
                                        ALU.add).then_inc(eps_done[which], 1)
                need(pool, eps_done[which], n + 1)
                nc.gpsimd.tensor_tensor(rstd[which][:, :], var_eps[which][:, :], neg_half[0:half_rows, :],
                                        ALU.pow).then_inc(rstd_done[which], 1)

            def inverse_norm(n):
                need(pool, squared, 3 * n + 3)
                nc.gpsimd.tensor_tensor(rnorm[:, :], ssq[:, :], neg_half[0:half_rows, :],
                                        ALU.pow).then_inc(rnorm_done, 1)

            def hid_lo(m, c):
                need(pool, hid_hi, HC * m + c + 1)
                nc.gpsimd.tensor_tensor(hidT[1][:, c, :], hid[c % 2][:, :], hidT[0][:, c, :].bitcast(F32),
                                        ALU.subtract).then_inc(hid_split, 1)

            move_pixels(0, 0)
            pool.wait_ge(w_loaded[3], 16)
            nc.gpsimd.tensor_copy(flat(we)[0], wstage[1][:, :]).then_inc(we_hi, 1)
            pool.wait_ge(we_hi, 1)
            nc.gpsimd.tensor_tensor(flat(we)[1], wstage[1][:, :], flat(we)[0].bitcast(F32),
                                    ALU.subtract).then_inc(we_split, 1)
            inverse_std(0, 0)

            def body(k, first=False, last=False):
                for u in range(2):
                    n = 2 * k + u
                    m = n - 1
                    ff = not (first and u == 0)
                    ahead = not (last and u == 1)
                    if ff:
                        for c in (0, 1, 2):
                            hid_lo(m, c)
                    inverse_norm(n)
                    if ff:
                        hid_lo(m, 3)
                    if ahead:
                        inverse_std(0, n + 1)
                    inverse_std(1, n)
                    if ff:
                        hid_lo(m, 4)
                        hid_lo(m, 5)
                    if u == 0 and not last:
                        move_pixels(k + 1, WEIGHT_GROUPS + FILLS if first else
                                    use_of(k, 1, MIDDLE, "fill5") + 1 - PER_BODY)

            body(0, first=True)
            with pool.Fori(1, pairs - 1) as k:
                body(k)
            body(pairs - 1, last=True)
            for c in range(HC):
                hid_lo(images - 1, c)

        @block.tensor
        def _(pe):
            def mm3(dst, left, right, start, stop):
                nc.tensor.matmul(dst, left[0], right[0], start=start, stop=False)
                nc.tensor.matmul(dst, left[1], right[0], start=False, stop=False)
                return nc.tensor.matmul(dst, left[0], right[1], start=False, stop=stop)

            def transpose_group(use, blocks):
                need(pe, tp_split, use - 1)
                at = 0
                for src in blocks:
                    rows = src.shape[0]
                    done = nc.tensor.transpose(tp[use % 2][0:src.shape[1], at:at + rows], src,
                                               ident[0:rows, 0:rows])
                    at += rows
                done.then_inc(transposed, 1)

            def fill(j, use, bank):
                lo, hi = FILL[j % 3]
                need(pe, tp_split, use - 1)
                for g in range(lo, hi):
                    src = pix[:, g, (j // 3) * HALF:(j // 3 + 1) * HALF]
                    done = nc.tensor.transpose(tp[bank][:, (g - lo) * px_rows:(g - lo + 1) * px_rows], src,
                                               ident[0:px_rows, 0:px_rows])
                done.then_inc(transposed, 1)

            def embed(par, bank, patches_ready):
                need(pe, tp_split, patches_ready)
                for t in range(2):
                    dst = ab[bank][0:half_rows, t * dim:(t + 1) * dim]
                    for c in range(channels):
                        for half in range(2):
                            at = (par * channels + c) * patches + t * half_rows
                            done = mm3(dst, [p[:, half, at:at + half_rows] for p in patT],
                                       [w[:, 2 * c + half, :] for w in we],
                                       c == 0 and half == 0, c == channels - 1 and half == 1)
                done.then_inc(embedded, 1)

            def transpose_tokens(src, f, use, bank):
                need(pe, tp_split, use - 1)
                for t in range(T):
                    done = nc.tensor.transpose(tp[bank][:, FIRST[t]:FIRST[t] + ROWS[t]],
                                               src[0:ROWS[t], t, f * P:(f + 1) * P],
                                               ident[0:ROWS[t], 0:ROWS[t]])
                done.then_inc(transposed, 1)

            def project(n, x_ready):
                need(pe, tp_split, x_ready)
                for f in range(DC):
                    need(pe, y_done, 3 * n - 1 + f)
                    for c in range(DC):
                        done = mm3(ab[1 + f][:, 0:wide], [w[:, c, f * P:(f + 1) * P] for w in wqk],
                                   [t[:, c, :] for t in xT], c == 0, c == DC - 1)
                    done.then_inc(projected, 1)

            def values(n):
                for t in range(T):
                    if t == 0:
                        need(pe, h_added, n + 1)
                    else:
                        need(pe, proj_split, 2 * n + t)
                    for c in range(DC):
                        done = mm3(ab[t][0:ROWS[t], 0:dim], [q[:, c, FIRST[t]:FIRST[t] + ROWS[t]] for q in xT],
                                   [w[:, c, :] for w in wvT], c == 0, c == DC - 1)
                    done.then_inc(valued, 1)

            def scores(n):
                need(pe, proj_split, 2 * n + 2)
                for t in range(T):
                    need(pe, v_split, 3 * n + t + 1)
                    for c in range(DC):
                        done = mm3(ab[t][0:ROWS[t], 0:wide], [q[:, c, FIRST[t]:FIRST[t] + ROWS[t]] for q in tT],
                                   [q[:, c, :] for q in xT], c == 0, c == DC - 1)
                    done.then_inc(scored, 1)

            def transpose_probs(n, j, use, bank):
                need(pe, tp_split, use - 1)
                for t in range(T):
                    if j == 0:
                        need(pe, exped, 3 * n + t + 1)
                    done = nc.tensor.transpose(tp[bank][0:ROWS[j], FIRST[t]:FIRST[t] + ROWS[t]],
                                               probs[0:ROWS[t], t, FIRST[j]:FIRST[j] + ROWS[j]],
                                               ident[0:ROWS[t], 0:ROWS[t]])
                done.then_inc(transposed, 1)

            def attend(n, probs_ready):
                need(pe, tp_split, probs_ready)
                for t in range(T):
                    for j in range(T):
                        done = mm3(ab[t][0:ROWS[t], 0:dim],
                                   [q[0:ROWS[j], j, FIRST[t]:FIRST[t] + ROWS[t]] for q in pT],
                                   [q[0:ROWS[j], j, :] for q in v], j == 0, j == T - 1)
                    done.then_inc(attended, 1)

            def gate_up(m, c):
                g, u = fb[(2 * c) % 3], fb[(2 * c + 1) % 3]
                if c >= 2:
                    need(pe, hid_done, HC * m + c - 1)
                else:
                    need(pe, final, 3 * m - 2 if c == 0 else 3 * m)
                for d in range(DC):
                    done = mm3(g[:, 0:wide], [w[:, d, c * P:(c + 1) * P] for w in wgT],
                               [q[:, d, :] for q in zT], d == 0, d == DC - 1)
                done.then_inc(gate_done, 1)
                if c >= 1:
                    need(pe, gated, HC * m + c)
                else:
                    need(pe, final, 3 * m - 1)
                for d in range(DC):
                    done = mm3(u[:, 0:wide], [w[:, d, c * P:(c + 1) * P] for w in wuT],
                               [q[:, d, :] for q in zT], d == 0, d == DC - 1)
                done.then_inc(up_done, 1)

            def down(m):
                for t in range(T):
                    for c in range(HC):
                        if t == 0:
                            need(pe, hid_split, HC * m + (5 if c == 0 else c + 1))
                        if t == 1 and c == 0:
                            need(pe, gated, HC * m + HC)
                        if t == 2 and c == 0:
                            need(pe, hid_done, HC * m + HC)
                        done = mm3(fb[t][0:ROWS[t], 0:dim], [q[:, c, FIRST[t]:FIRST[t] + ROWS[t]] for q in hidT],
                                   [w[:, c, :] for w in wdT], c == 0, c == HC - 1)
                    done.then_inc(downed, 1)

            pe.wait_ge(ident_set, 2)
            pe.wait_ge(w_loaded[0], 16)
            pe.wait_ge(w_loaded[1], 16)
            st = wstage[0]
            for d in range(DC):
                for e in range(DC):
                    done = nc.tensor.matmul(tp[0][:, d * dim:(d + 1) * dim],
                                            st[:, e * dim + d * P:e * dim + (d + 1) * P],
                                            st[:, (DC + e) * dim:(DC + e + 1) * dim],
                                            start=e == 0, stop=e == DC - 1)
            done.then_inc(transposed, 1)
            pe.wait_ge(w_loaded[2], 16)
            transpose_group(1, [st[:, (2 * DC + e) * dim + c * P:(2 * DC + e) * dim + (c + 1) * P]
                                for c in range(DC) for e in range(DC)])
            pe.wait_ge(consts_set, 1)
            for j in range(FILLS):
                pe.wait_ge(px_moved, j // 3 + 1)
                fill(j, 2 + j, j % 2)
            pe.wait_ge(we_split, 1)
            embed(0, 0, 2 + FILLS)
            use = 2 + FILLS
            for i, (rows, cols) in enumerate(((HC, DC), (HC, DC), (DC, HC))):
                pe.wait_ge(w_float, i + 1)
                blocks = [wstage[(i + 1) % 2][:, (r * cols + c) * P:(r * cols + c + 1) * P]
                          for c in range(cols) for r in range(rows)]
                for g in range(3):
                    transpose_group(use, blocks[4 * g:4 * g + 4])
                    use += 1
            assert use == WEIGHT_GROUPS + FILLS
            pe.wait_ge(normed[0], 3)
            for f in range(DC):
                transpose_tokens(xn[0], f, use + f, (use + f) % 2)
            project(0, BEFORE)
            values(0)

            def body(k, first=False, last=False):
                for u in range(2):
                    n = 2 * k + u
                    m = n - 1
                    ff = not (first and u == 0)
                    ahead = not (last and u == 1)
                    refill = u == 1 and not last

                    def use(name):
                        return use_of(k, u, last, name)

                    def bank(name):
                        return bank_of(u, last, name)

                    def next_fill(j):
                        need(pe, px_moved, 2 * (k + 1) + j // 3 + 1)
                        fill(j, use(f"fill{j}"), bank(f"fill{j}"))

                    scores(n)
                    need(pe, tp_split, k * PER_BODY + BEFORE + u * PER_SLOT[0])
                    if ff:
                        gate_up(m, 0)
                    if refill:
                        next_fill(0)
                    if ff:
                        gate_up(m, 1)
                    if refill:
                        next_fill(1)
                    for j in range(T):
                        transpose_probs(n, j, use(f"probs{j}"), bank(f"probs{j}"))
                    if refill:
                        next_fill(2)
                    if ff:
                        gate_up(m, 2)
                    if refill:
                        next_fill(3)
                    attend(n, use("probs2") + 1)
                    if refill:
                        next_fill(4)
                        next_fill(5)
                    if ff:
                        gate_up(m, 3)
                    if ahead:
                        need(pe, y_done, 3 * n + 1)
                        embed(1 - u, 0, use("fill5") + 1 if refill else 0)
                    if ff:
                        gate_up(m, 4)
                        gate_up(m, 5)
                    if ahead:
                        need(pe, normed[0], 3 * (n + 1) + 3)
                        for f in range(DC):
                            transpose_tokens(xn[1 - u], f, use(f"x{f}"), bank(f"x{f}"))
                    if ff:
                        down(m)
                    if ahead:
                        project(n + 1, use("x1") + 1)
                        values(n + 1)
                    need(pe, normed[1], 3 * n + 3)
                    for f in range(DC):
                        transpose_tokens(z, f, use(f"z{f}"), bank(f"z{f}"))

            body(0, first=True)
            with pe.Fori(1, pairs - 1) as k:
                body(k)
            body(pairs - 1, last=True)
            pe.wait_ge(tp_split, use_of(pairs - 1, 1, LAST, "z1") + 1)
            for c in range(HC):
                gate_up(images - 1, c)
            down(images - 1)

        @block.scalar
        def _(act):
            def hi_part(dst, src, after, count, signal):
                need(act, after, count)
                nc.scalar.activation(dst, src, ACT.Copy).then_inc(signal, 1)

            def fill_view(t, j):
                lo, hi = FILL[j % 3]
                return t[:, j // 3, :].rearrange("p (q g) -> p q g", g=grid)[:, :, lo:hi]

            def fill_bank(bank, j):
                lo, hi = FILL[j % 3]
                return tp[bank][:, 0:(hi - lo) * px_rows].rearrange("p (g q) -> p q g", q=px_rows)

            def fill_hi(j, use, bank):
                hi_part(fill_view(patT[0], j), fill_bank(bank, j), transposed, use + 1, tp_hi)

            def tokens_hi(dst, f, use, bank):
                hi_part(dst[:, f, 0:tokens], tp[bank][:, 0:tokens], transposed, use + 1, tp_hi)

            def projection_hi(n):
                for f in range(DC):
                    hi_part(tT[0][:, f, :], ab[1 + f][:, 0:tokens], projected, 2 * n + f + 1, proj_hi)
                for t in range(T):
                    hi_part(v[0][0:ROWS[t], t, :], ab[t][0:ROWS[t], 0:dim], valued, 3 * n + t + 1, v_hi)

            def tanh_hi(m, c):
                need(act, gated, HC * m + c - 1)
                need(act, gate_done, HC * m + c + 1)
                nc.scalar.activation(th[c % 2][:, :], fb[(2 * c) % 3][:, 0:tokens], ACT.Tanh,
                                     scale=0.5 * INT_SCALE).then_inc(tanh_done, 1)
                hi_part(hidT[0][:, c, :], hid[c % 2][:, :], hid_done, HC * m + c + 1, hid_hi)

            groups = [wqk, wvT]
            for i, dst in enumerate(groups):
                hi_part(flat(dst)[0], tp[i % 2][:, :], transposed, i + 1, tp_hi)
            for j in range(FILLS):
                fill_hi(j, 2 + j, j % 2)
            use = 2 + FILLS
            for dst in (wgT, wuT, wdT):
                for g in range(3):
                    hi_part(flat(dst)[0][:, g * 512:(g + 1) * 512], tp[use % 2][:, :], transposed, use + 1, tp_hi)
                    use += 1
            act.wait_ge(consts_set, 1)
            for f in range(DC):
                tokens_hi(xT[0], f, use + f, (use + f) % 2)
            projection_hi(0)

            def body(k, first=False, last=False):
                for u in range(2):
                    n = 2 * k + u
                    m = n - 1
                    ff = not (first and u == 0)
                    ahead = not (last and u == 1)
                    refill = u == 1 and not last

                    def use(name):
                        return use_of(k, u, last, name)

                    def bank(name):
                        return bank_of(u, last, name)

                    def next_fill(j):
                        fill_hi(j, use(f"fill{j}"), bank(f"fill{j}"))

                    for t in range(T):
                        need(act, maxed, 3 * n + t + 1)
                        nc.scalar.activation(probs[0:ROWS[t], t, :], ab[t][0:ROWS[t], 0:tokens], ACT.Exp,
                                             bias=nmax[0:ROWS[t], t:t + 1],
                                             accum_out=den[0:ROWS[t], t:t + 1]).then_inc(exped, 1)
                    if ff:
                        tanh_hi(m, 0)
                    if refill:
                        next_fill(0)
                    if ff:
                        tanh_hi(m, 1)
                    if refill:
                        next_fill(1)
                    for j in range(T):
                        hi_part(pT[0][0:ROWS[j], j, :], tp[bank(f"probs{j}")][0:ROWS[j], 0:tokens],
                                transposed, use(f"probs{j}") + 1, tp_hi)
                    if refill:
                        next_fill(2)
                    if ff:
                        tanh_hi(m, 2)
                    if refill:
                        next_fill(3)
                    for t in range(T):
                        need(act, y_done, 3 * n + t + 1)
                        nc.scalar.activation(ysq[0:ROWS[t], t, :], y[0:ROWS[t], t, :], ACT.Square,
                                             accum_out=ssq[0:ROWS[t], t:t + 1]).then_inc(squared, 1)
                    if refill:
                        next_fill(4)
                        next_fill(5)
                    if ff:
                        for c in (3, 4, 5):
                            tanh_hi(m, c)
                    if ahead:
                        for f in range(DC):
                            tokens_hi(xT[0], f, use(f"x{f}"), bank(f"x{f}"))
                        projection_hi(n + 1)
                    for f in range(DC):
                        tokens_hi(zT[0], f, use(f"z{f}"), bank(f"z{f}"))

            body(0, first=True)
            with act.Fori(1, pairs - 1) as k:
                body(k)
            body(pairs - 1, last=True)
            for c in range(HC):
                tanh_hi(images - 1, c)

        @block.vector
        def _(dve):
            def lo_part(dst, src, hi, after, count, signal):
                need(dve, after, count)
                nc.vector.tensor_tensor(dst, src, hi.bitcast(F32), ALU.subtract).then_inc(signal, 1)

            def fill_lo(j, use, bank):
                lo, hi = FILL[j % 3]
                views = [t[:, j // 3, :].rearrange("p (q g) -> p q g", g=grid)[:, :, lo:hi] for t in patT]
                src = tp[bank][:, 0:(hi - lo) * px_rows].rearrange("p (g q) -> p q g", q=px_rows)
                lo_part(views[1], src, views[0], tp_hi, use + 1, tp_split)

            def tokens_lo(dst, f, use, bank):
                lo_part(dst[1][:, f, 0:tokens], tp[bank][:, 0:tokens], dst[0][:, f, 0:tokens],
                        tp_hi, use + 1, tp_split)

            def projection_lo(n):
                for f in range(DC):
                    lo_part(tT[1][:, f, :], ab[1 + f][:, 0:tokens], tT[0][:, f, :], proj_hi, 2 * n + f + 1,
                            proj_split)
                for t in range(T):
                    r = ROWS[t]
                    lo_part(v[1][0:r, t, :], ab[t][0:r, 0:dim], v[0][0:r, t, :], v_hi, 3 * n + t + 1, v_split)

            def statistics(which, src, n, after, counts):
                for t in range(T):
                    need(dve, after[t], counts[t])
                    nc.vector.bn_stats(stats[which][0:ROWS[t], t, :], src[0:ROWS[t], t, :]
                                       ).then_inc(bn_done[which], 1)
                for t in range(T):
                    need_apart(dve, bn_done[which], 3 * n + t + 1)
                    nc.vector.bn_aggr(mv[which][0:ROWS[t], t, :], stats[which][0:ROWS[t], t, :]
                                      ).then_inc(mv_done[which], 1)

            def normalise(which, dst, src, n):
                need(dve, rstd_done[which], n + 1)
                for t in range(T):
                    r = ROWS[t]
                    nc.vector.tensor_scalar(dst[0:r, t, :], src[0:r, t, :], mv[which][0:r, t, 0:1],
                                            rstd[which][0:r, t:t + 1], ALU.subtract, ALU.mult
                                            ).then_inc(normed[which], 1)

            def add_positions(n, par, text_count):
                need(dve, embedded, n + 1)
                nc.vector.tensor_tensor(h[par][:, 0:2, :], ab[0][0:half_rows, :].rearrange("p (t d) -> p t d", t=2),
                                        pos[:, :, :], ALU.add).then_inc(h_added, 1)
                statistics(0, h[par], n, (h_added, h_added, text_loaded[par]), (n + 1, n + 1, text_count))

            def gate(m, c):
                need(dve, tanh_done, HC * m + c + 1)
                nc.vector.scalar_tensor_tensor(ga[c % 2][:, :], th[c % 2][:, :], 1.0,
                                               fb[(2 * c) % 3][:, 0:tokens], ALU.add, ALU.mult
                                               ).then_inc(gated, 1)
                need(dve, gated, HC * m + c + 1)
                need(dve, hid_split, HC * m + c - 1)
                need(dve, up_done, HC * m + c + 1)
                nc.vector.tensor_tensor(hid[c % 2][:, :], ga[c % 2][:, :], fb[(2 * c + 1) % 3][:, 0:tokens],
                                        ALU.mult).then_inc(hid_done, 1)

            def finish(m, par, stores):
                need(dve, stored[par], stores)
                for t in range(T):
                    r = ROWS[t]
                    need(dve, downed, 3 * m + t + 1)
                    nc.vector.scalar_tensor_tensor(res[par][0:r, t, :], fb[t][0:r, 0:dim],
                                                   0.5 * INT_SCALE ** 3, h2[par][0:r, t, :], ALU.mult, ALU.add
                                                   ).then_inc(final, 1)

            dve.wait_ge(pos_loaded, 32)
            for t in range(2):
                nc.vector.tensor_tensor(pos[:, t, :], pos[:, t, :], bias[:, :], ALU.add).then_inc(pos_set, 1)
            for i, dst in enumerate((wqk, wvT)):
                lo_part(flat(dst)[1], tp[i % 2][:, :], flat(dst)[0], tp_hi, i + 1, tp_split)
            for j in range(FILLS):
                fill_lo(j, 2 + j, j % 2)
            dve.wait_ge(we_split, 1)
            dve.wait_ge(w_loaded[4], 16)
            nc.vector.tensor_copy(wstage[1][:, :], wint[:, :]).then_inc(w_float, 1)
            dve.wait_ge(pos_set, 2)
            dve.wait_ge(consts_set, 1)
            add_positions(0, 0, 16)
            normalise(0, xn[0], h[0], 0)
            dve.wait_ge(w_loaded[5], 16)
            nc.vector.tensor_copy(wstage[0][:, :], wint[:, :]).then_inc(w_float, 1)
            use = 2 + FILLS
            for i, dst in enumerate((wgT, wuT, wdT)):
                if i == 1:
                    dve.wait_ge(w_loaded[6], 16)
                    nc.vector.tensor_copy(wstage[1][:, :], wint[:, :]).then_inc(w_float, 1)
                for g in range(3):
                    lo_part(flat(dst)[1][:, g * 512:(g + 1) * 512], tp[use % 2][:, :],
                            flat(dst)[0][:, g * 512:(g + 1) * 512], tp_hi, use + 1, tp_split)
                    use += 1
            for f in range(DC):
                tokens_lo(xT, f, use + f, (use + f) % 2)
            projection_lo(0)

            def body(k, first=False, last=False):
                for u in range(2):
                    n = 2 * k + u
                    m = n - 1
                    ff = not (first and u == 0)
                    ahead = not (last and u == 1)
                    refill = u == 1 and not last

                    def use(name):
                        return use_of(k, u, last, name)

                    def bank(name):
                        return bank_of(u, last, name)

                    def next_fill(j):
                        fill_lo(j, use(f"fill{j}"), bank(f"fill{j}"))

                    for t in range(T):
                        r = ROWS[t]
                        need(dve, scored, 3 * n + t + 1)
                        nc.vector.tensor_reduce(nmax[0:r, t:t + 1], ab[t][0:r, 0:tokens], AX_X, ALU.max,
                                                negate=True).then_inc(maxed, 1)
                    if ff:
                        gate(m, 0)
                    if refill:
                        next_fill(0)
                    if ff:
                        gate(m, 1)
                    if refill:
                        next_fill(1)
                    for j in range(T):
                        r = ROWS[j]
                        lo_part(pT[1][0:r, j, :], tp[bank(f"probs{j}")][0:r, 0:tokens], pT[0][0:r, j, :],
                                tp_hi, use(f"probs{j}") + 1, tp_split)
                    if refill:
                        next_fill(2)
                    need(dve, exped, 3 * n + 3)
                    nc.vector.reciprocal(rden[:, :], den[:, :]).then_inc(rden_done, 1)
                    if ff:
                        gate(m, 2)
                    if refill:
                        next_fill(3)
                    need(dve, rden_done, n + 1)
                    for t in range(T):
                        r = ROWS[t]
                        need(dve, attended, 3 * n + t + 1)
                        nc.vector.scalar_tensor_tensor(y[0:r, t, :], ab[t][0:r, 0:dim], rden[0:r, t:t + 1],
                                                       xn[u][0:r, t, :], ALU.mult, ALU.add).then_inc(y_done, 1)
                    if refill:
                        next_fill(4)
                        next_fill(5)
                    if ff:
                        gate(m, 3)
                    if ahead:
                        add_positions(n + 1, 1 - u, 16 * (k + 1) + (16 if u == 1 else 0))
                    need(dve, rnorm_done, n + 1)
                    for t in range(T):
                        r = ROWS[t]
                        nc.vector.scalar_tensor_tensor(h2[u][0:r, t, :], y[0:r, t, :], rnorm[0:r, t:t + 1],
                                                       h[u][0:r, t, :], ALU.mult, ALU.add).then_inc(h2_done, 1)
                    statistics(1, h2[u], n, (h2_done,) * 3, [3 * n + t + 1 for t in range(T)])
                    if ff:
                        gate(m, 4)
                    if ahead:
                        normalise(0, xn[1 - u], h[1 - u], n + 1)
                    if ff:
                        gate(m, 5)
                    normalise(1, z, h2[u], n)
                    if ahead:
                        for f in range(DC):
                            tokens_lo(xT, f, use(f"x{f}"), bank(f"x{f}"))
                    if ff:
                        finish(m, 1 - u, STORES * (k + u))
                    if ahead:
                        projection_lo(n + 1)
                    for f in range(DC):
                        tokens_lo(zT, f, use(f"z{f}"), bank(f"z{f}"))

            body(0, first=True)
            with dve.Fori(1, pairs - 1) as k:
                body(k)
            body(pairs - 1, last=True)
            for c in range(HC):
                gate(images - 1, c)
            finish(images - 1, 1, STORES * pairs)


_INS = ["x", "txt", "L0_tok_W_embed", "L0_tok_b_embed", "L0_tok_pos_embed", "L0_attn_Wq", "L0_attn_Wk",
        "L0_attn_Wv", "L0_ffn_w_gate", "L0_ffn_w_up", "L0_ffn_w_down"]


def kernel(**inputs):
    import numpy as np
    import concourse.bacc as bacc
    from concourse.bass_utils import run_bass_kernel_spmd

    nc = bacc.Bacc("TRN2", target_bir_lowering=False, num_devices=1)
    arrays, args = {}, []
    for name in _INS:
        a = np.ascontiguousarray(inputs[name])
        arrays[f"in_{name}"] = a
        args.append(nc.dram_tensor(f"in_{name}", a.shape, mybir.dt.from_np(a.dtype), kind="ExternalInput").ap())
    images, _, _, _ = inputs["x"].shape
    tokens = inputs["txt"].shape[1] + inputs["L0_tok_pos_embed"].shape[1]
    dim = inputs["txt"].shape[2]
    args.append(nc.dram_tensor("out_h", (images, tokens, dim), F32, kind="ExternalOutput").ap())
    fusion_layer(nc, *args)
    r = run_bass_kernel_spmd(nc, [arrays], core_ids=[0])
    return r.results[0]["out_h"]
```

```python
from contextlib import ExitStack

import concourse.bass as bass
from concourse import mybir

F32 = mybir.dt.float32
F32R = mybir.dt.float32r
I32 = mybir.dt.int32
ALU = mybir.AluOpType
ACT = mybir.ActivationFunctionType
AX_X = mybir.AxisListType.X

P = 128
EPS = 1e-5
INT_SCALE = 1.0 / 127.0


def fusion_layer(nc, x, txt, w_embed, b_embed, pos_embed, wq, wk, wv, w_gate, w_up, w_down, out):
    images, channels, side, _ = x.shape
    text = txt.shape[1]
    dim = wq.shape[0]
    hidden = w_gate.shape[0]
    patches = pos_embed.shape[1]
    grid = side // 16
    patch = side // grid
    tokens = patches + text
    wide = tokens + 1
    half_rows = patches // 2
    ROWS = (half_rows, half_rows, text)
    FIRST = (0, half_rows, patches)
    T = len(ROWS)
    DC = dim // P
    HC = hidden // P
    STORES = 2 * 16
    PAIR = 2
    pairs = images // PAIR
    px_rows = PAIR * channels * grid
    px_cols = patch * side
    HALF = patch * patch // 2
    FILL = ((0, 5), (5, 10), (10, grid))
    FILLS = 2 * len(FILL)
    HIDS = 4
    MOVES = 4

    x_rows = x.rearrange("b c (g i) w -> (b c g) (i w)", i=patch)
    out_rows = out.rearrange("b s d -> (b s) d")
    txt_rows = txt.rearrange("b s d -> (b s) d")

    LAST, MIDDLE = True, False

    def bank_order(u, last):
        early, late = [], []
        if not last:
            early, late = [f"fill{j}" for j in range(3, FILLS)], [f"fill{j}" for j in range(3)]
        if u == 0:
            order = ["h", "probs0", "probs1", "probs2", "x0", "x1"] + late
        else:
            order = early + ["probs0", "probs1", "probs2"]
            if not last:
                order += ["h", "x0", "x1"]
        return order + ["z0", "z1", "out0", "out1"]

    W_USES = 2 + 3 * 3
    BEFORE = W_USES + FILLS + 1 + DC
    PER_BODY = len(bank_order(0, MIDDLE)) + len(bank_order(1, MIDDLE))
    assert PER_BODY % 2 == 0

    def slot_start(k, u, last, first=False):
        start = BEFORE if first and u == 0 else BEFORE - 2
        return k * PER_BODY + start + u * len(bank_order(0, last))

    def use_of(k, u, last, name, first=False):
        return slot_start(k, u, last, first) + bank_order(u, last).index(name)

    def bank_of(u, last, name):
        return (BEFORE + u * len(bank_order(0, last)) + bank_order(u, last).index(name)) % 2

    def split_order(u, last):
        return [name for name in bank_order(u, last) if name not in ("h", "out0", "out1")]

    HI_BEFORE = BEFORE - 1
    HI_BODY = len(split_order(0, MIDDLE)) + len(split_order(1, MIDDLE))

    def hi_count(k, u, last, name):
        return k * HI_BODY + HI_BEFORE + u * len(split_order(0, last)) + split_order(u, last).index(name) + 1

    with ExitStack() as ctx:
        def sb(name, shape, dt=F32):
            return ctx.enter_context(nc.sbuf_tensor(name, shape, dt))

        def sem(name):
            return ctx.enter_context(nc.semaphore(name))

        def split(name, shape):
            return sb(name + "_hi", shape, F32R), sb(name + "_lo", shape, F32R)

        raw = sb("raw_pixels", [px_rows, px_cols])
        pix = sb("patch_pixels", [px_rows, grid, patch * patch])
        patT = split("patches_T", [P, 2, PAIR * channels * patches])
        we = split("w_embed", [P, 2 * channels, dim])
        wqk = split("w_qk", [P, DC, dim])
        wvT = split("wv_T", [P, DC, dim])
        wgT = split("w_gate_T", [P, DC, hidden])
        wuT = split("w_up_T", [P, DC, hidden])
        wdT = split("w_down_T", [P, HC, dim])
        pos = sb("pos_bias", [half_rows, 2, dim])
        bias = sb("bias_rows", [half_rows, dim])
        ident = sb("identity", [P, P])
        eps = sb("eps", [P, T])
        neg_half = sb("minus_half", [P, T])
        h = [sb(f"h{i}", [half_rows, T, dim]) for i in range(2)]
        xn = [sb(f"x_norm{i}", [half_rows, T, dim]) for i in range(2)]
        xT = split("x_T", [P, DC, wide])
        tT = split("xw_T", [P, DC, tokens])
        xs = split("x_split", [half_rows, T, dim])
        uT = split("probs_x_T", [P, DC, tokens])
        embT = sb("embedding_T", [P, DC, PAIR, patches])
        downT = sb("down_T", [P, DC, tokens])
        probs = sb("probs", [half_rows, T, tokens])
        pT = split("probs_T", [half_rows, T, wide])
        y = sb("y", [half_rows, T, dim])
        ysq = sb("y_squared", [half_rows, T, dim])
        h2_both = sb("h_mid", [P, 2, T, dim])
        h2 = [h2_both[0:half_rows, i] for i in range(2)]
        z = sb("z_norm", [half_rows, T, dim])
        zT = split("z_T", [P, DC, wide])
        th = [sb(f"tanh{i}", [P, tokens]) for i in range(2)]
        ga = [sb(f"gated{i}", [P, tokens]) for i in range(2)]
        hid = [sb(f"hid{i}", [P, tokens]) for i in range(HIDS)]
        hidT = split("hid_T", [P, HC, wide])
        res_both = sb("result", [P, 2, T, dim])
        res = [res_both[0:half_rows, i] for i in range(2)]
        assert 2 * T * dim == DC * hidden
        wstage = [h2_both[:].rearrange("p a t d -> p (a t d)"), sb("w_stage", [P, DC * hidden])]
        wint = res_both[:].rearrange("p a t d -> p (a t d)").bitcast(I32)
        stats = [sb(f"bn{i}", [half_rows, T, 6]) for i in range(2)]
        mv = [sb(f"mean_var{i}", [half_rows, T, 2]) for i in range(2)]
        var_eps = [sb(f"var_eps{i}", [half_rows, T]) for i in range(2)]
        rstd = [sb(f"rstd{i}", [half_rows, T]) for i in range(2)]
        nmax = sb("minus_max", [half_rows, T])
        den = sb("denominator", [half_rows, T])
        rden = sb("one_over_denominator", [half_rows, T])
        neg_mean = sb("minus_mean", [half_rows, T])
        shift = sb("minus_mean_rstd", [half_rows, T])
        neg_one = sb("minus_one", [P, T])
        ssq = sb("y_square_sum", [half_rows, T])
        lo_max = sb("w_lo_max", [P, T])
        lo_any = sb("w_lo_any", [P, 2])
        lo_flag = sb("w_lo_flag", [1, 1], I32)
        rnorm = sb("one_over_norm", [half_rows, T])

        def psum(name):
            return ctx.enter_context(nc.psum_tensor(name, [P, 512], F32))

        tp = [psum(f"transposing{i}") for i in range(2)]
        ab = [psum(f"attention{i}") for i in range(3)]
        fb = [psum(f"feed_forward{i}") for i in range(3)]

        consts_set = sem("consts_set")
        ident_set = sem("ident_set")
        w_loaded = [sem(f"w_loaded{i}") for i in range(7)]
        pos_loaded = sem("pos_loaded")
        w_float = sem("w_float")
        we_hi = sem("we_hi")
        we_split = sem("we_split")
        pos_set = sem("pos_set")
        px_loaded = sem("px_loaded")
        px_moved = sem("px_moved")
        text_loaded = [sem(f"text_loaded{i}") for i in range(2)]
        stored = [sem(f"stored{i}") for i in range(2)]
        transposed = sem("transposed")
        tp_hi = sem("transposed_hi")
        tp_split = sem("transposed_split")
        embedded = sem("embedded")
        emb_out = sem("emb_out")
        bn_done = [sem(f"bn_done{i}") for i in range(2)]
        mv_done = [sem(f"mv_done{i}") for i in range(2)]
        eps_done = [sem(f"eps_done{i}") for i in range(2)]
        rstd_done = [sem(f"rstd_done{i}") for i in range(2)]
        normed = [sem(f"normed{i}") for i in range(2)]
        projected = sem("projected")
        proj_hi = sem("proj_hi")
        proj_split = sem("proj_split")
        negated = sem("negated")
        shifted = sem("shifted")
        x_hi = sem("x_hi")
        x_split = sem("x_split_done")
        weighted = sem("weighted")
        u_hi = sem("u_hi")
        u_split = sem("u_split")
        scored = sem("scored")
        maxed = sem("maxed")
        exped = sem("exped")
        rden_done = sem("rden_done")
        attended = sem("attended")
        y_done = sem("y_done")
        squared = sem("squared")
        rnorm_done = sem("rnorm_done")
        h2_done = sem("h2_done")
        gate_done = sem("gate_done")
        up_done = sem("up_done")
        tanh_done = sem("tanh_done")
        gated = sem("gated")
        hid_done = sem("hid_done")
        hid_hi = sem("hid_hi")
        hid_split = sem("hid_split")
        downed = sem("downed")
        down_out = sem("down_out")
        w_lo_seen = sem("w_lo_seen")
        passed = {nc.vector: sem("dve_passed"), nc.gpsimd: sem("pool_passed")}
        final = sem("final")

        def need(eng, semaphore, value):
            if not (isinstance(value, int) and value <= 0):
                eng.wait_ge(semaphore, value)

        def need_apart(eng, semaphore, value):
            need(eng, semaphore, value)
            eng.sem_inc(passed[eng], 1)

        def HID(m_par, c):
            return (m_par * HC + c) % HIDS

        FILL_NEEDS = [(1 if hi <= grid // 2 else 2) + 2 * half for half in range(2) for _, hi in FILL]

        def flat(pair_of_parts):
            return [t[:].rearrange("p a b -> p (a b)") for t in pair_of_parts]

        block = ctx.enter_context(nc.Block())

        @block.sync
        def _(sp):
            sp.dma_start(raw[:, :], x_rows[0:px_rows, :]).then_inc(px_loaded, 16)
            for par in range(2):
                sp.sem_inc(stored[par], STORES)
            sp.dma_start(wstage[0][:, 0:DC * dim].rearrange("p (c d) -> p c d", c=DC),
                         wq.rearrange("(c p) d -> p c d", p=P)).then_inc(w_loaded[0], 16)
            sp.dma_start(wstage[0][:, DC * dim:2 * DC * dim].rearrange("p (c d) -> p c d", c=DC),
                         wk.rearrange("(c p) d -> p c d", p=P)).then_inc(w_loaded[1], 16)
            sp.dma_start(wstage[0][:, 2 * DC * dim:3 * DC * dim].rearrange("p (c d) -> p c d", c=DC),
                         wv.rearrange("(c p) d -> p c d", p=P)).then_inc(w_loaded[2], 16)
            sp.dma_start(wstage[1][:, :].rearrange("p (c d) -> p c d", d=dim),
                         w_embed.rearrange("(c p) d -> p c d", p=P)).then_inc(w_loaded[3], 16)
            sp.dma_start(pos[:, :, :], pos_embed.rearrange("o (t p) d -> p (o t) d", p=half_rows)
                         ).then_inc(pos_loaded, 16)
            sp.dma_start(bias[:, :], b_embed.rearrange("(o d) -> o d", o=1).to_broadcast([half_rows, dim])
                         ).then_inc(pos_loaded, 16)
            sp.dma_start(h[0][0:text, 2, :], txt_rows[0:text, :]).then_inc(text_loaded[0], 16)
            sp.dma_start(wint[:, :].rearrange("p (c d) -> p c d", d=dim),
                         w_gate.rearrange("(c p) d -> p c d", p=P)).then_inc(w_loaded[4], 16)
            sp.wait_ge(w_float, 1)
            sp.dma_start(wint[:, :].rearrange("p (c d) -> p c d", d=dim),
                         w_up.rearrange("(c p) d -> p c d", p=P)).then_inc(w_loaded[5], 16)
            sp.wait_ge(w_float, 2)
            sp.dma_start(wint[:, :].rearrange("p (c h) -> p c h", h=hidden),
                         w_down.rearrange("(c p) h -> p c h", p=P)).then_inc(w_loaded[6], 16)

            def store(m, par, results):
                need(sp, tp_split, results)
                sp.dma_start(out_rows[bass.ds(m * tokens, patches), :].rearrange("(t p) d -> p t d", p=half_rows),
                             res[par][:, 0:2, :]).then_inc(stored[par], 16)
                sp.dma_start(out_rows[bass.ds(m * tokens + patches, text), :],
                             res[par][0:text, 2, :]).then_inc(stored[par], 16)

            def body(k, first=False, last=False):
                for u in range(2):
                    n = 2 * k + u
                    if u == 0 and not last:
                        need(sp, px_moved, MOVES * (k + 1))
                        sp.dma_start(raw[:, :], x_rows[bass.ds((k + 1) * px_rows, px_rows), :]
                                     ).then_inc(px_loaded, 16)
                    if not (last and u == 1):
                        need(sp, h2_done, 3 * n)
                        sp.dma_start(h[1 - u][0:text, 2, :], txt_rows[bass.ds((n + 1) * text, text), :]
                                     ).then_inc(text_loaded[1 - u], 16)
                    if not (first and u == 0):
                        store(n - 1, 1 - u, use_of(k, u, last, "out1") + 1)

            body(0, first=True)
            with sp.Fori(1, pairs - 1) as k:
                body(k)
            body(pairs - 1, last=True)
            store(images - 1, 1, use_of(pairs - 1, 1, LAST, "out1") + 3)
            for par in range(2):
                sp.wait_ge(stored[par], STORES * (pairs + 1))

        @block.gpsimd
        def _(pool):
            nc.gpsimd.memset(ident[:, :], 0.0).then_inc(ident_set, 1)
            pool.wait_ge(ident_set, 1)
            nc.gpsimd.affine_select(out=ident[:, :], in_=ident[:, :], compare_op=ALU.not_equal, fill=1.0,
                                    base=0, pattern=[[-1, P]], channel_multiplier=1).then_inc(ident_set, 1)
            nc.gpsimd.memset(eps[:, :], EPS)
            nc.gpsimd.memset(neg_half[:, :], -0.5)
            nc.gpsimd.memset(neg_one[:, :], -1.0)
            for t in (xT[0], xT[1], zT[0], zT[1], pT[0], pT[1], hidT[0], hidT[1]):
                nc.gpsimd.memset(t[:, :, tokens:wide].bitcast(F32), 0.0)
            for t in (den, ssq, mv[0], mv[1]):
                last_set = nc.gpsimd.memset(t[:], 1.0)
            last_set.then_inc(consts_set, 1)

            def inverse_std(which, n):
                need(pool, mv_done[which], 3 * n + 3)
                nc.gpsimd.tensor_tensor(var_eps[which][:, :], mv[which][:, :, 1], eps[0:half_rows, :],
                                        ALU.add).then_inc(eps_done[which], 1)
                need(pool, eps_done[which], n + 1)
                nc.gpsimd.tensor_tensor(rstd[which][:, :], var_eps[which][:, :], neg_half[0:half_rows, :],
                                        ALU.pow).then_inc(rstd_done[which], 1)

            def inverse_std_and_shift(n):
                need(pool, mv_done[0], 3 * n + 3)
                nc.gpsimd.tensor_tensor(neg_mean[:, :], mv[0][:, :, 0], neg_one[0:half_rows, :],
                                        ALU.mult).then_inc(negated, 1)
                inverse_std(0, n)
                need(pool, negated, n + 1)
                need(pool, rstd_done[0], n + 1)
                nc.gpsimd.tensor_tensor(shift[:, :], neg_mean[:, :], rstd[0][:, :], ALU.mult
                                        ).then_inc(shifted, 1)

            def normalise_x(n, par):
                need_apart(pool, shifted, n + 1)
                for t in range(T):
                    r = ROWS[t]
                    nc.gpsimd.tensor_scalar(xn[par][0:r, t, :], h[par][0:r, t, :], rstd[0][0:r, t:t + 1],
                                            shift[0:r, t:t + 1], ALU.mult, ALU.add).then_inc(normed[0], 1)

            def x_lo(n, par):
                for t in range(T):
                    r = ROWS[t]
                    need(pool, x_hi, 3 * n + t + 1)
                    nc.gpsimd.tensor_tensor(xs[1][0:r, t, :], xn[par][0:r, t, :], xs[0][0:r, t, :].bitcast(F32),
                                            ALU.subtract).then_inc(x_split, 1)

            def inverse_norm(n):
                need(pool, squared, 3 * n + 3)
                nc.gpsimd.tensor_tensor(rnorm[:, :], ssq[:, :], neg_half[0:half_rows, :],
                                        ALU.pow).then_inc(rnorm_done, 1)

            def hid_lo(m, m_par, c):
                need(pool, hid_hi, HC * m + c + 1)
                nc.gpsimd.tensor_tensor(hidT[1][:, c, 0:tokens], hid[HID(m_par, c)][:, :], hidT[0][:, c, 0:tokens].bitcast(F32),
                                        ALU.subtract).then_inc(hid_split, 1)

            pool.wait_ge(w_loaded[3], 16)
            nc.gpsimd.tensor_copy(flat(we)[0], wstage[1][:, :]).then_inc(we_hi, 1)
            pool.wait_ge(we_hi, 1)
            nc.gpsimd.tensor_tensor(flat(we)[1], wstage[1][:, :], flat(we)[0].bitcast(F32),
                                    ALU.subtract).then_inc(we_split, 1)
            inverse_std_and_shift(0)
            normalise_x(0, 0)
            x_lo(0, 0)
            pool.wait_ge(w_lo_seen, 4)
            nc.gpsimd.partition_all_reduce(lo_any[:, 1:2], lo_any[:, 0:1], P,
                                           bass.bass_isa.ReduceOp.max).then_inc(w_lo_seen, 1)

            def body(k, first=False, last=False):
                for u in range(2):
                    n = 2 * k + u
                    m, m_par = n - 1, 1 - u
                    ff = not (first and u == 0)
                    ahead = not (last and u == 1)
                    if ff:
                        hid_lo(m, m_par, 0)
                        hid_lo(m, m_par, 1)
                        hid_lo(m, m_par, 2)
                    if ahead:
                        inverse_std_and_shift(n + 1)
                        normalise_x(n + 1, 1 - u)
                    if ff:
                        hid_lo(m, m_par, 3)
                    inverse_norm(n)
                    if ff:
                        hid_lo(m, m_par, 4)
                        hid_lo(m, m_par, 5)
                    inverse_std(1, n)
                    if ahead:
                        x_lo(n + 1, 1 - u)

            body(0, first=True)
            with pool.Fori(1, pairs - 1) as k:
                body(k)
            body(pairs - 1, last=True)
            for c in range(HC):
                hid_lo(images - 1, 1, c)

        @block.tensor
        def _(pe):
            def mm3(dst, left, right, start, stop):
                nc.tensor.matmul(dst, left[0], right[0], start=start, stop=False)
                nc.tensor.matmul(dst, left[1], right[0], start=False, stop=False)
                return nc.tensor.matmul(dst, left[0], right[1], start=False, stop=stop)

            def transpose_group(use, blocks):
                need(pe, tp_split, use - 1)
                at = 0
                for src in blocks:
                    rows = src.shape[0]
                    done = nc.tensor.transpose(tp[use % 2][0:src.shape[1], at:at + rows], src,
                                               ident[0:rows, 0:rows])
                    at += rows
                done.then_inc(transposed, 1)

            def fill(j, use, bank):
                lo, hi = FILL[j % 3]
                need(pe, tp_split, use - 1)
                for g in range(lo, hi):
                    src = pix[:, g, (j // 3) * HALF:(j // 3 + 1) * HALF]
                    done = nc.tensor.transpose(tp[bank][:, (g - lo) * px_rows:(g - lo + 1) * px_rows], src,
                                               ident[0:px_rows, 0:px_rows])
                done.then_inc(transposed, 1)

            def embed(patches_ready):
                need(pe, tp_split, patches_ready)
                for f in range(DC):
                    dst = ab[2 - f][:, 0:PAIR * patches].rearrange("p (b s) -> p b s", b=PAIR)
                    for c in range(channels):
                        for half in range(2):
                            done = mm3(dst, [w[:, 2 * c + half, f * P:(f + 1) * P] for w in we],
                                       [p[:, half, :].rearrange("p (b s) -> p b s", b=PAIR)
                                        [:, :, c * patches:(c + 1) * patches] for p in patT],
                                       c == 0 and half == 0, c == channels - 1 and half == 1)
                    done.then_inc(embedded, 1)

            def transpose_embedding(par, outs, use, bank):
                need(pe, emb_out, outs)
                need(pe, tp_split, use - 1)
                for t in range(2):
                    for f in range(DC):
                        done = nc.tensor.transpose(tp[bank][0:half_rows, t * dim + f * P:t * dim + (f + 1) * P],
                                                   embT[:, f, par, t * half_rows:(t + 1) * half_rows], ident[:, :])
                done.then_inc(transposed, 1)

            def transpose_tokens(src, f, use, bank):
                need(pe, tp_split, use - 1)
                for t in range(T):
                    done = nc.tensor.transpose(tp[bank][:, FIRST[t]:FIRST[t] + ROWS[t]],
                                               src[0:ROWS[t], t, f * P:(f + 1) * P],
                                               ident[0:ROWS[t], 0:ROWS[t]])
                done.then_inc(transposed, 1)

            def project(n, x_ready):
                need(pe, tp_split, x_ready)
                for f in range(DC):
                    need(pe, y_done, 3 * n - 2 + f)
                    for c in range(DC):
                        done = mm3(ab[f][:, 0:wide], [w[:, c, f * P:(f + 1) * P] for w in wqk],
                                   [t[:, c, :] for t in xT], c == 0, c == DC - 1)
                    done.then_inc(projected, 1)

            def scores(n):
                need(pe, proj_split, 2 * n + 2)
                for t in range(T):
                    if t == 2:
                        need(pe, y_done, 3 * n)
                    for c in range(DC):
                        done = mm3(ab[t][0:ROWS[t], 0:wide], [q[:, c, FIRST[t]:FIRST[t] + ROWS[t]] for q in tT],
                                   [q[:, c, :] for q in xT], c == 0, c == DC - 1)
                    done.then_inc(scored, 1)

            def transpose_probs(n, j, use, bank):
                need(pe, tp_split, use - 1)
                for t in range(T):
                    if j == 0:
                        need(pe, exped, 3 * n + t + 1)
                    done = nc.tensor.transpose(tp[bank][0:ROWS[j], FIRST[t]:FIRST[t] + ROWS[t]],
                                               probs[0:ROWS[t], t, FIRST[j]:FIRST[j] + ROWS[j]],
                                               ident[0:ROWS[t], 0:ROWS[t]])
                done.then_inc(transposed, 1)

            def weigh(n, probs_ready, outs):
                need(pe, tp_split, probs_ready)
                need(pe, x_split, 3 * n + 3)
                for f in range(DC):
                    if f == 1 and outs is not None:
                        need(pe, emb_out, outs)
                    for j in range(T):
                        done = mm3(ab[f][:, 0:wide], [q[0:ROWS[j], j, f * P:(f + 1) * P] for q in xs],
                                   [q[0:ROWS[j], j, :] for q in pT], j == 0, j == T - 1)
                    done.then_inc(weighted, 1)

            def attend(n):
                need(pe, u_split, 2 * n + 2)
                for t in range(T):
                    for f in range(DC):
                        done = mm3(ab[t][0:ROWS[t], 0:dim], [q[:, f, FIRST[t]:FIRST[t] + ROWS[t]] for q in uT],
                                   [w[:, f, :] for w in wvT], f == 0, f == DC - 1)
                    done.then_inc(attended, 1)

            def mm_int(dst, weights, right, general, start, stop):
                if general:
                    return mm3(dst, weights, right, start, stop)
                nc.tensor.matmul(dst, weights[0], right[0], start=start, stop=False)
                return nc.tensor.matmul(dst, weights[0], right[1], start=False, stop=stop)

            def gate_up(m, c, general):
                g, u = fb[(2 * c) % 3], fb[(2 * c + 1) % 3]
                if c == 0:
                    need(pe, down_out, 2 * m - 1)
                elif c == 1:
                    need(pe, hid_done, HC * m)
                else:
                    need(pe, hid_done, HC * m + c - 1)
                for d in range(DC):
                    done = mm_int(g[:, 0:wide], [w[:, d, c * P:(c + 1) * P] for w in wgT],
                                  [q[:, d, :] for q in zT], general, d == 0, d == DC - 1)
                done.then_inc(gate_done, 1)
                if c == 0:
                    need(pe, down_out, 2 * m)
                else:
                    need(pe, gated, HC * m + c)
                for d in range(DC):
                    done = mm_int(u[:, 0:wide], [w[:, d, c * P:(c + 1) * P] for w in wuT],
                                  [q[:, d, :] for q in zT], general, d == 0, d == DC - 1)
                done.then_inc(up_done, 1)

            def down(m, f, general):
                if f == 0:
                    need(pe, hid_done, HC * m + HC - 1)
                else:
                    need(pe, gated, HC * m + HC)
                for c in range(HC):
                    if f == 0:
                        need(pe, hid_split, HC * m + c + 1)
                    done = mm_int(fb[f][:, 0:wide], [w[:, c, f * P:(f + 1) * P] for w in wdT],
                                  [q[:, c, :] for q in hidT], general, c == 0, c == HC - 1)
                done.then_inc(downed, 1)

            def transpose_down(m, uses, banks):
                for i, tiles in enumerate(((0, 1), (2,))):
                    need(pe, tp_split, uses[i] - 1)
                    for t in tiles:
                        for f in range(DC):
                            if t == 0:
                                need(pe, down_out, 2 * m + f + 1)
                            at = t % 2 * dim + f * P
                            done = nc.tensor.transpose(tp[banks[i]][0:ROWS[t], at:at + P],
                                                       downT[:, f, FIRST[t]:FIRST[t] + ROWS[t]], ident[:, :])
                    done.then_inc(transposed, 1)

            pe.wait_ge(ident_set, 2)
            pe.wait_ge(w_loaded[0], 16)
            pe.wait_ge(w_loaded[1], 16)
            st = wstage[0]
            for d in range(DC):
                for e in range(DC):
                    done = nc.tensor.matmul(tp[0][:, d * dim:(d + 1) * dim],
                                            st[:, e * dim + d * P:e * dim + (d + 1) * P],
                                            st[:, (DC + e) * dim:(DC + e + 1) * dim],
                                            start=e == 0, stop=e == DC - 1)
            done.then_inc(transposed, 1)
            pe.wait_ge(w_loaded[2], 16)
            transpose_group(1, [st[:, (2 * DC + e) * dim + c * P:(2 * DC + e) * dim + (c + 1) * P]
                                for c in range(DC) for e in range(DC)])
            pe.wait_ge(consts_set, 1)
            for j in range(FILLS):
                pe.wait_ge(px_moved, FILL_NEEDS[j])
                fill(j, 2 + j, j % 2)
            pe.wait_ge(we_split, 1)
            embed(2 + FILLS)
            transpose_embedding(0, DC, 2 + FILLS, (2 + FILLS) % 2)
            use = 2 + FILLS + 1
            for i, (rows, cols) in enumerate(((HC, DC), (HC, DC), (DC, HC))):
                pe.wait_ge(w_float, i + 1)
                blocks = [wstage[(i + 1) % 2][:, (r * cols + c) * P:(r * cols + c + 1) * P]
                          for c in range(cols) for r in range(rows)]
                for g in range(3):
                    transpose_group(use, blocks[4 * g:4 * g + 4])
                    use += 1
            assert use == W_USES + FILLS + 1
            pe.wait_ge(normed[0], 3)
            for f in range(DC):
                transpose_tokens(xn[0], f, use + f, (use + f) % 2)
            project(0, BEFORE)

            def body(k, general, first=False, last=False):
                for u in range(2):
                    n = 2 * k + u
                    m = n - 1
                    ff = not (first and u == 0)
                    ahead = not (last and u == 1)
                    refill = not last

                    def use(name):
                        return use_of(k, u, last, name, first)

                    def bank(name):
                        return bank_of(u, last, name)

                    def next_fill(j):
                        if refill:
                            need(pe, px_moved, MOVES * (k + 1) + FILL_NEEDS[j])
                            fill(j, use(f"fill{j}"), bank(f"fill{j}"))

                    def hidden(c):
                        if ff:
                            gate_up(m, c, general)

                    def embedding_back():
                        transpose_embedding(1 - u, DC * (k + 1 + u), use("h"), bank("h"))

                    def probs_back(*js):
                        for j in js:
                            transpose_probs(n, j, use(f"probs{j}"), bank(f"probs{j}"))

                    scores(n)
                    if u == 1:
                        next_fill(3)
                        next_fill(4)
                    if ff:
                        need(pe, tp_split, slot_start(k, u, last) - (0 if first else 2))
                    hidden(0)
                    if u == 0:
                        embedding_back()
                        probs_back(0, 1)
                        hidden(1)
                    else:
                        next_fill(5)
                        hidden(1)
                        probs_back(0, 1)
                        if ahead:
                            embed(use("fill5") + 1)
                    probs_back(2)
                    hidden(2)
                    if u == 1 and ahead:
                        embedding_back()
                    weigh(n, use("probs2") + 1, DC * (k + 2) if u == 1 and ahead else None)
                    hidden(3)
                    attend(n)
                    hidden(4)
                    if ahead:
                        need(pe, normed[0], 3 * (n + 1) + 3)
                        for f in range(DC):
                            transpose_tokens(xn[1 - u], f, use(f"x{f}"), bank(f"x{f}"))
                    hidden(5)
                    if u == 0:
                        next_fill(0)
                    if ahead:
                        project(n + 1, use("x1") + 1)
                    if u == 0:
                        next_fill(1)
                    if ff:
                        down(m, 0, general)
                    if u == 0:
                        next_fill(2)
                    if ff:
                        down(m, 1, general)
                    need(pe, normed[1], 3 * n + 3)
                    for f in range(DC):
                        transpose_tokens(z, f, use(f"z{f}"), bank(f"z{f}"))
                    if ff:
                        transpose_down(m, (use("out0"), use("out1")), (bank("out0"), bank("out1")))

            def pipeline(general):
                body(0, general, first=True)
                with pe.Fori(1, pairs - 1) as k:
                    body(k, general)
                body(pairs - 1, general, last=True)
                end = use_of(pairs - 1, 1, LAST, "out1") + 1
                pe.wait_ge(tp_split, end - 2)
                for c in range(HC):
                    gate_up(images - 1, c, general)
                for f in range(DC):
                    down(images - 1, f, general)
                transpose_down(images - 1, (end, end + 1), (end % 2, (end + 1) % 2))

            pe.wait_ge(w_lo_seen, 6)
            general = pe.value_load(lo_flag[0:1, 0:1], min_val=0, max_val=1)
            with pe.If(general != 0):
                pipeline(True)
            with pe.Else():
                pipeline(False)

        @block.scalar
        def _(act):
            def hi_part(dst, src, after, count, signal):
                need(act, after, count)
                nc.scalar.activation(dst, src, ACT.Copy).then_inc(signal, 1)

            def fill_view(t, j):
                lo, hi = FILL[j % 3]
                return t[:, j // 3, :].rearrange("p (q g) -> p q g", g=grid)[:, :, lo:hi]

            def fill_bank(bank, j):
                lo, hi = FILL[j % 3]
                return tp[bank][:, 0:(hi - lo) * px_rows].rearrange("p (g q) -> p q g", q=px_rows)

            def fill_hi(j, use, bank):
                hi_part(fill_view(patT[0], j), fill_bank(bank, j), transposed, use + 1, tp_hi)

            def tokens_hi(dst, f, use, bank):
                hi_part(dst[:, f, 0:tokens], tp[bank][:, 0:tokens], transposed, use + 1, tp_hi)

            def move_pixels(pair, steps):
                for step in steps:
                    half, side_ = step // 2, step % 2
                    cols = slice(side_ * grid // 2, (side_ + 1) * grid // 2)
                    need(act, px_loaded, 16 * pair + 16)
                    nc.scalar.activation(
                        pix[:, cols, half * HALF:(half + 1) * HALF].rearrange("r g (i j) -> r g i j", j=patch),
                        raw[:, :].rearrange("r (i g j) -> r g i j", i=patch, j=patch)
                        [:, cols, half * patch // 2:(half + 1) * patch // 2, :], ACT.Copy).then_inc(px_moved, 1)

            def embedding_out(pair):
                for f in range(DC):
                    need(act, embedded, DC * pair + f + 1)
                    nc.scalar.activation(embT[:, f, :, :],
                                         ab[2 - f][:, 0:PAIR * patches].rearrange("p (b s) -> p b s", b=PAIR),
                                         ACT.Copy).then_inc(emb_out, 1)

            def x_parts(n, par):
                need(act, weighted, 2 * n)
                for t in range(T):
                    hi_part(xs[0][0:ROWS[t], t, :], xn[par][0:ROWS[t], t, :], normed[0], 3 * n + t + 1, x_hi)

            def projection_hi(n):
                for f in range(DC):
                    hi_part(tT[0][:, f, :], ab[f][:, 0:tokens], projected, 2 * n + f + 1, proj_hi)

            def weighed_hi(n):
                for f in range(DC):
                    hi_part(uT[0][:, f, :], ab[f][:, 0:tokens], weighted, 2 * n + f + 1, u_hi)

            def tanh(m, c):
                need(act, gated, HC * m + c - 1)
                need(act, gate_done, HC * m + c + 1)
                nc.scalar.activation(th[c % 2][:, :], fb[(2 * c) % 3][:, 0:tokens], ACT.Tanh,
                                     scale=0.5 * INT_SCALE).then_inc(tanh_done, 1)

            def hidden_hi(m, m_par, c):
                hi_part(hidT[0][:, c, 0:tokens], hid[HID(m_par, c)][:, :], hid_done, HC * m + c + 1, hid_hi)

            def downs_out(m):
                for f in range(DC):
                    need(act, downed, 2 * m + f + 1)
                    nc.scalar.activation(downT[:, f, :], fb[f][:, 0:tokens], ACT.Copy).then_inc(down_out, 1)

            move_pixels(0, range(MOVES))
            for i, dst in enumerate((wqk, wvT)):
                hi_part(flat(dst)[0], tp[i % 2][:, :], transposed, i + 1, tp_hi)
            for j in range(FILLS):
                fill_hi(j, 2 + j, j % 2)
            act.wait_ge(consts_set, 1)
            embedding_out(0)
            x_parts(0, 0)
            use = 2 + FILLS + 1
            for dst in (wgT, wuT, wdT):
                for g in range(3):
                    hi_part(flat(dst)[0][:, g * 512:(g + 1) * 512], tp[use % 2][:, :], transposed, use + 1, tp_hi)
                    use += 1
            for f in range(DC):
                tokens_hi(xT[0], f, use + f, (use + f) % 2)
            projection_hi(0)

            def body(k, first=False, last=False):
                for u in range(2):
                    n = 2 * k + u
                    m, m_par = n - 1, 1 - u
                    ff = not (first and u == 0)
                    ahead = not (last and u == 1)
                    refill = not last

                    def use(name):
                        return use_of(k, u, last, name, first)

                    def bank(name):
                        return bank_of(u, last, name)

                    def next_fill(j):
                        if refill:
                            fill_hi(j, use(f"fill{j}"), bank(f"fill{j}"))

                    def probs_hi(j):
                        hi_part(pT[0][0:ROWS[j], j, 0:tokens], tp[bank(f"probs{j}")][0:ROWS[j], 0:tokens],
                                transposed, use(f"probs{j}") + 1, tp_hi)

                    def exponentials(t):
                        need(act, maxed, 3 * n + t + 1)
                        nc.scalar.activation(probs[0:ROWS[t], t, :], ab[t][0:ROWS[t], 0:tokens], ACT.Exp,
                                             bias=nmax[0:ROWS[t], t:t + 1],
                                             accum_out=den[0:ROWS[t], t:t + 1]).then_inc(exped, 1)

                    def squares(t):
                        need(act, y_done, 3 * n + t + 1)
                        nc.scalar.activation(ysq[0:ROWS[t], t, :], y[0:ROWS[t], t, :], ACT.Square,
                                             accum_out=ssq[0:ROWS[t], t:t + 1]).then_inc(squared, 1)

                    def hidden_tanh(c):
                        if ff:
                            tanh(m, c)

                    def hidden_out(c):
                        if ff:
                            hidden_hi(m, m_par, c)

                    for t in range(T):
                        exponentials(t)
                    if u == 1:
                        next_fill(3)
                        next_fill(4)
                    hidden_tanh(0)
                    if u == 1:
                        next_fill(5)
                        hidden_tanh(1)
                        hidden_out(0)
                    probs_hi(0)
                    probs_hi(1)
                    if u == 0:
                        hidden_out(0)
                        hidden_tanh(1)
                    hidden_out(1)
                    if u == 1 and ahead:
                        embedding_out(k + 1)
                    probs_hi(2)
                    hidden_tanh(2)
                    hidden_out(2)
                    weighed_hi(n)
                    hidden_tanh(3)
                    hidden_out(3)
                    if u == 0 and refill:
                        move_pixels(k + 1, (0,))
                    for t in range(T):
                        squares(t)
                    hidden_tanh(4)
                    hidden_out(4)
                    if ahead:
                        for f in range(DC):
                            tokens_hi(xT[0], f, use(f"x{f}"), bank(f"x{f}"))
                    hidden_tanh(5)
                    if u == 0 and refill:
                        move_pixels(k + 1, (1,))
                    hidden_out(5)
                    if u == 0:
                        next_fill(0)
                    if ahead:
                        projection_hi(n + 1)
                    if u == 0 and refill:
                        next_fill(1)
                        move_pixels(k + 1, (2,))
                        next_fill(2)
                        move_pixels(k + 1, (3,))
                    if ff:
                        downs_out(m)
                    for f in range(DC):
                        tokens_hi(zT[0], f, use(f"z{f}"), bank(f"z{f}"))
                    if ahead:
                        x_parts(n + 1, 1 - u)

            body(0, first=True)
            with act.Fori(1, pairs - 1) as k:
                body(k)
            body(pairs - 1, last=True)
            for c in range(HC):
                tanh(images - 1, c)
                hidden_hi(images - 1, 1, c)
            downs_out(images - 1)

        @block.vector
        def _(dve):
            def lo_part(dst, src, hi, after, count, signal):
                need(dve, after, count)
                nc.vector.tensor_tensor(dst, src, hi.bitcast(F32), ALU.subtract).then_inc(signal, 1)

            def fill_lo(j, his, bank):
                lo, hi = FILL[j % 3]
                views = [t[:, j // 3, :].rearrange("p (q g) -> p q g", g=grid)[:, :, lo:hi] for t in patT]
                src = tp[bank][:, 0:(hi - lo) * px_rows].rearrange("p (g q) -> p q g", q=px_rows)
                lo_part(views[1], src, views[0], tp_hi, his, tp_split)

            def tokens_lo(dst, f, his, bank):
                lo_part(dst[1][:, f, 0:tokens], tp[bank][:, 0:tokens], dst[0][:, f, 0:tokens], tp_hi, his, tp_split)

            def projection_lo(n):
                for f in range(DC):
                    lo_part(tT[1][:, f, :], ab[f][:, 0:tokens], tT[0][:, f, :], proj_hi, 2 * n + f + 1, proj_split)

            def weighed_lo(n):
                for f in range(DC):
                    lo_part(uT[1][:, f, :], ab[f][:, 0:tokens], uT[0][:, f, :], u_hi, 2 * n + f + 1, u_split)

            def statistics(which, src, n, after, counts):
                for t in range(T):
                    need(dve, after[t], counts[t])
                    nc.vector.bn_stats(stats[which][0:ROWS[t], t, :], src[0:ROWS[t], t, :]
                                       ).then_inc(bn_done[which], 1)
                for t in range(T):
                    need_apart(dve, bn_done[which], 3 * n + t + 1)
                    nc.vector.bn_aggr(mv[which][0:ROWS[t], t, :], stats[which][0:ROWS[t], t, :]
                                      ).then_inc(mv_done[which], 1)

            def normalise(which, dst, src, n):
                need(dve, rstd_done[which], n + 1)
                for t in range(T):
                    r = ROWS[t]
                    nc.vector.tensor_scalar(dst[0:r, t, :], src[0:r, t, :], mv[which][0:r, t, 0:1],
                                            rstd[which][0:r, t:t + 1], ALU.subtract, ALU.mult
                                            ).then_inc(normed[which], 1)

            def add_positions(par, use, bank):
                need(dve, transposed, use + 1)
                nc.vector.tensor_tensor(h[par][:, 0:2, :], tp[bank][0:half_rows, :].rearrange("p (t d) -> p t d", t=2),
                                        pos[:, :, :], ALU.add).then_inc(tp_split, 1)

            def h_statistics(n, par, text_count, use):
                statistics(0, h[par], n, (tp_split, tp_split, text_loaded[par]), (use + 1, use + 1, text_count))

            def gate(m, m_par, c):
                need(dve, tanh_done, HC * m + c + 1)
                nc.vector.scalar_tensor_tensor(ga[c % 2][:, :], th[c % 2][:, :], 1.0,
                                               fb[(2 * c) % 3][:, 0:tokens], ALU.add, ALU.mult
                                               ).then_inc(gated, 1)
                need(dve, gated, HC * m + c + 1)
                need(dve, hid_split, HC * m + c + 1 - HIDS)
                need(dve, up_done, HC * m + c + 1)
                nc.vector.tensor_tensor(hid[HID(m_par, c)][:, :], ga[c % 2][:, :], fb[(2 * c + 1) % 3][:, 0:tokens],
                                        ALU.mult).then_inc(hid_done, 1)

            def finish(m, par, stores, uses, banks):
                need(dve, stored[par], stores)
                for i, (t0, t1) in enumerate(((0, 2), (2, 3))):
                    r = ROWS[t0]
                    need(dve, transposed, uses[i] + 1)
                    nc.vector.scalar_tensor_tensor(
                        res[par][0:r, t0:t1, :].rearrange("p t d -> p (t d)"), tp[banks[i]][0:r, 0:(t1 - t0) * dim],
                        0.5 * INT_SCALE ** 3, h2[par][0:r, t0:t1, :].rearrange("p t d -> p (t d)"),
                        ALU.mult, ALU.add).then_inc(tp_split, 1)

            dve.wait_ge(pos_loaded, 32)
            for t in range(2):
                nc.vector.tensor_tensor(pos[:, t, :], pos[:, t, :], bias[:, :], ALU.add).then_inc(pos_set, 1)
            for i, dst in enumerate((wqk, wvT)):
                lo_part(flat(dst)[1], tp[i % 2][:, :], flat(dst)[0], tp_hi, i + 1, tp_split)
            for j in range(FILLS):
                fill_lo(j, 3 + j, j % 2)
            dve.wait_ge(we_split, 1)
            dve.wait_ge(w_loaded[4], 16)
            nc.vector.tensor_copy(wstage[1][:, :], wint[:, :]).then_inc(w_float, 1)
            dve.wait_ge(pos_set, 2)
            dve.wait_ge(consts_set, 1)
            add_positions(0, 2 + FILLS, (2 + FILLS) % 2)
            h_statistics(0, 0, 16, 2 + FILLS)
            dve.wait_ge(w_loaded[5], 16)
            nc.vector.tensor_copy(wstage[0][:, :], wint[:, :]).then_inc(w_float, 1)
            use = 2 + FILLS + 1
            for i, dst in enumerate((wgT, wuT, wdT)):
                if i == 1:
                    dve.wait_ge(w_loaded[6], 16)
                    nc.vector.tensor_copy(wstage[1][:, :], wint[:, :]).then_inc(w_float, 1)
                for g in range(3):
                    lo_part(flat(dst)[1][:, g * 512:(g + 1) * 512], tp[use % 2][:, :],
                            flat(dst)[0][:, g * 512:(g + 1) * 512], tp_hi, use, tp_split)
                    use += 1
            for i, w in enumerate((wgT, wuT, wdT)):
                dve.wait_ge(tp_split, use)
                nc.vector.tensor_reduce(lo_max[:, i:i + 1], flat(w)[1].bitcast(F32), AX_X, ALU.max,
                                        apply_absolute_value=True).then_inc(w_lo_seen, 1)
            dve.wait_ge(w_lo_seen, 3)
            nc.vector.tensor_reduce(lo_any[:, 0:1], lo_max[:, :], AX_X, ALU.max).then_inc(w_lo_seen, 1)
            for f in range(DC):
                tokens_lo(xT, f, use + f, (use + f) % 2)
            projection_lo(0)
            dve.wait_ge(w_lo_seen, 5)
            nc.vector.tensor_scalar(lo_flag[0:1, 0:1], lo_any[0:1, 1:2], 0.0, None, ALU.is_gt
                                    ).then_inc(w_lo_seen, 1)

            def body(k, first=False, last=False):
                for u in range(2):
                    n = 2 * k + u
                    m, m_par = n - 1, 1 - u
                    ff = not (first and u == 0)
                    ahead = not (last and u == 1)
                    refill = not last

                    def use(name):
                        return use_of(k, u, last, name, first)

                    def bank(name):
                        return bank_of(u, last, name)

                    def his(name):
                        return hi_count(k, u, last, name)

                    def next_fill(j):
                        if refill:
                            fill_lo(j, his(f"fill{j}"), bank(f"fill{j}"))

                    def probs_lo(j):
                        r = ROWS[j]
                        lo_part(pT[1][0:r, j, 0:tokens], tp[bank(f"probs{j}")][0:r, 0:tokens],
                                pT[0][0:r, j, 0:tokens], tp_hi, his(f"probs{j}"), tp_split)

                    def hidden(c):
                        if ff:
                            gate(m, m_par, c)

                    for t in range(T):
                        r = ROWS[t]
                        need(dve, scored, 3 * n + t + 1)
                        nc.vector.tensor_reduce(nmax[0:r, t:t + 1], ab[t][0:r, 0:tokens], AX_X, ALU.max,
                                                negate=True).then_inc(maxed, 1)
                    if u == 1:
                        next_fill(3)
                        next_fill(4)
                    hidden(0)
                    if u == 0:
                        add_positions(1, use("h"), bank("h"))
                    else:
                        next_fill(5)
                        hidden(1)
                    probs_lo(0)
                    probs_lo(1)
                    if u == 0:
                        hidden(1)
                    probs_lo(2)
                    need(dve, exped, 3 * n + 3)
                    nc.vector.reciprocal(rden[:, :], den[:, :]).then_inc(rden_done, 1)
                    hidden(2)
                    if u == 1 and ahead:
                        add_positions(0, use("h"), bank("h"))
                    if ahead:
                        h_statistics(n + 1, 1 - u, 16 * (k + 1 + u), use("h"))
                    weighed_lo(n)
                    hidden(3)
                    need(dve, rden_done, n + 1)
                    for t in range(T):
                        r = ROWS[t]
                        need(dve, attended, 3 * n + t + 1)
                        nc.vector.scalar_tensor_tensor(y[0:r, t, :], ab[t][0:r, 0:dim], rden[0:r, t:t + 1],
                                                       xn[u][0:r, t, :], ALU.mult, ALU.add).then_inc(y_done, 1)
                    hidden(4)
                    need(dve, rnorm_done, n + 1)
                    for t in range(T):
                        r = ROWS[t]
                        nc.vector.scalar_tensor_tensor(h2[u][0:r, t, :], y[0:r, t, :], rnorm[0:r, t:t + 1],
                                                       h[u][0:r, t, :], ALU.mult, ALU.add).then_inc(h2_done, 1)
                    if ahead:
                        for f in range(DC):
                            tokens_lo(xT, f, his(f"x{f}"), bank(f"x{f}"))
                    statistics(1, h2[u], n, (h2_done,) * 3, [3 * n + t + 1 for t in range(T)])
                    hidden(5)
                    if u == 0:
                        next_fill(0)
                    if ahead:
                        projection_lo(n + 1)
                    if u == 0:
                        next_fill(1)
                    normalise(1, z, h2[u], n)
                    if u == 0:
                        next_fill(2)
                    for f in range(DC):
                        tokens_lo(zT, f, his(f"z{f}"), bank(f"z{f}"))
                    if ff:
                        finish(m, 1 - u, STORES * (k + u), (use("out0"), use("out1")), (bank("out0"), bank("out1")))

            body(0, first=True)
            with dve.Fori(1, pairs - 1) as k:
                body(k)
            body(pairs - 1, last=True)
            for c in range(HC):
                gate(images - 1, 1, c)
            end = use_of(pairs - 1, 1, LAST, "out1") + 1
            finish(images - 1, 1, STORES * pairs, (end, end + 1), (end % 2, (end + 1) % 2))


_INS = ["x", "txt", "L0_tok_W_embed", "L0_tok_b_embed", "L0_tok_pos_embed", "L0_attn_Wq", "L0_attn_Wk",
        "L0_attn_Wv", "L0_ffn_w_gate", "L0_ffn_w_up", "L0_ffn_w_down"]


def kernel(**inputs):
    import numpy as np
    import concourse.bacc as bacc
    from concourse.bass_utils import run_bass_kernel_spmd

    nc = bacc.Bacc("TRN2", target_bir_lowering=False, num_devices=1)
    arrays, args = {}, []
    for name in _INS:
        a = np.ascontiguousarray(inputs[name])
        arrays[f"in_{name}"] = a
        args.append(nc.dram_tensor(f"in_{name}", a.shape, mybir.dt.from_np(a.dtype), kind="ExternalInput").ap())
    images, _, _, _ = inputs["x"].shape
    tokens = inputs["txt"].shape[1] + inputs["L0_tok_pos_embed"].shape[1]
    dim = inputs["txt"].shape[2]
    args.append(nc.dram_tensor("out_h", (images, tokens, dim), F32, kind="ExternalOutput").ap())
    fusion_layer(nc, *args)
    r = run_bass_kernel_spmd(nc, [arrays], core_ids=[0])
    return r.results[0]["out_h"]
```

```python
from contextlib import ExitStack

import concourse.bass as bass
from concourse import mybir

F32 = mybir.dt.float32
F32R = mybir.dt.float32r
I32 = mybir.dt.int32
ALU = mybir.AluOpType
ACT = mybir.ActivationFunctionType
AX_X = mybir.AxisListType.X

P = 128
EPS = 1e-5
INT_SCALE = 1.0 / 127.0


def fusion_layer(nc, x, txt, w_embed, b_embed, pos_embed, wq, wk, wv, w_gate, w_up, w_down, out):
    images, channels, side, _ = x.shape
    text = txt.shape[1]
    dim = wq.shape[0]
    hidden = w_gate.shape[0]
    patches = pos_embed.shape[1]
    grid = side // 16
    patch = side // grid
    tokens = patches + text
    wide = tokens + 1
    half_rows = patches // 2
    ROWS = (half_rows, half_rows, text)
    TOKEN0 = (0, half_rows, patches)
    T = len(ROWS)
    DC = dim // P
    HC = hidden // P
    TEXT_LOADED = 16
    STORES = 2 * 16
    PAIR = 2
    pairs = images // PAIR
    px_rows = PAIR * channels * grid
    px_cols = patch * side
    HALF = patch * patch // 2
    FILL = ((0, 5), (5, 10), (10, grid))
    FILLS = 2 * len(FILL)
    HIDS = 4
    MOVES = 4

    x_rows = x.rearrange("b c (g i) w -> (b c g) (i w)", i=patch)
    out_rows = out.rearrange("b s d -> (b s) d")
    txt_rows = txt.rearrange("b s d -> (b s) d")

    ODD, EVEN, FIRST, SECOND = "odd", "even", "first", "second"
    ODD_LAST, EVEN_LAST, END = "odd_last", "even_last", "end"
    ODD_USES = ("z0", "z1", "probs0", "probs1", "probs2", "h", "out0",
              "out1", "fill0", "x0", "x1", "fill1", "fill2")
    EVEN_USES = ("z0", "z1", "out0", "h", "probs0", "probs1", "probs2",
              "fill3", "out1", "fill4", "fill5", "x0", "x1")

    def left(uses, *skipped):
        return [name for name in uses if not name.startswith(skipped)] if skipped else list(uses)

    USES = {ODD: left(ODD_USES), EVEN: left(EVEN_USES), FIRST: left(EVEN_USES, "out", "z"),
            SECOND: left(ODD_USES, "out"),
            ODD_LAST: left(ODD_USES, "fill"), EVEN_LAST: left(EVEN_USES, "fill"),
            END: left(ODD_USES, "fill", "h", "x")}
    HALF_FILLS = len(FILL)
    USE_WQK = FILLS
    USE_WV = USE_WQK + 1
    USE_H = USE_WV + 1
    USE_FILLS = USE_H + 1
    USE_GATE = USE_FILLS + HALF_FILLS
    USE_X = USE_GATE + 3
    USE_UP = USE_X + DC
    USE_DOWN = USE_UP + 3
    BEFORE = USE_DOWN + 3

    def offsets(before, uses):
        size = {kind: len(names) for kind, names in uses.items()}
        per_body = size[ODD] + size[EVEN]
        start = {FIRST: before, SECOND: before + size[FIRST] - per_body}
        start[ODD] = before + size[FIRST] + size[SECOND] + size[EVEN] - 2 * per_body
        start[EVEN] = start[ODD] + size[ODD]
        start[ODD_LAST] = start[ODD]
        start[EVEN_LAST] = start[ODD] + size[ODD_LAST]
        start[END] = start[EVEN_LAST] + size[EVEN_LAST] - per_body
        return start, per_body

    USE_START, PER_BODY = offsets(BEFORE, USES)
    SPLITS = {kind: left(names, "out", "h") for kind, names in USES.items()}
    HI_START, HI_BODY = offsets(BEFORE - 1, SPLITS)
    assert PER_BODY % 2 == 0

    class Slot:
        def __init__(self, kind, k):
            self.kind, self.k = kind, k
            self.ff = kind != FIRST
            self.ahead = kind != END
            self.refill = kind in (FIRST, SECOND, ODD, EVEN)
            self.outs = kind not in (FIRST, SECOND)
            self.start = k * PER_BODY + USE_START[kind]
            self.end = self.start + len(USES[kind])
            self.hi_end = k * HI_BODY + HI_START[kind] + len(SPLITS[kind])

        def use(self, name):
            return self.start + USES[self.kind].index(name)

        def bank(self, name):
            return (USE_START[self.kind] + USES[self.kind].index(name)) % 2

        def his(self, name):
            return self.k * HI_BODY + HI_START[self.kind] + SPLITS[self.kind].index(name) + 1

    with ExitStack() as ctx:
        def sb(name, shape, dt=F32):
            return ctx.enter_context(nc.sbuf_tensor(name, shape, dt))

        def sem(name):
            return ctx.enter_context(nc.semaphore(name))

        def split(name, shape):
            return sb(name + "_hi", shape, F32R), sb(name + "_lo", shape, F32R)

        raw = sb("raw_pixels", [px_rows, px_cols])
        pix = sb("patch_pixels", [px_rows, grid, patch * patch])
        patT = split("patches_T", [P, 2, PAIR * channels * patches])
        we = split("w_embed", [P, 2 * channels, dim])
        wqk = split("w_qk", [P, DC, dim])
        wvT = split("wv_T", [P, DC, dim])
        wgT = split("w_gate_T", [P, DC, hidden])
        wuT = split("w_up_T", [P, DC, hidden])
        wdT = split("w_down_T", [P, HC, dim])
        pos = sb("pos_bias", [half_rows, 2, dim])
        bias = sb("bias_rows", [half_rows, dim])
        ident = sb("identity", [P, P])
        eps = sb("eps", [P, T])
        neg_half = sb("minus_half", [P, T])
        h = [sb(f"h{i}", [half_rows, T, dim]) for i in range(2)]
        xn = [sb(f"x_norm{i}", [half_rows, T, dim]) for i in range(2)]
        xT = split("x_T", [P, DC, wide])
        tT = split("xw_T", [P, DC, tokens])
        xs = split("x_split", [half_rows, T, dim])
        uT = split("probs_x_T", [P, DC, tokens])
        embT = sb("embedding_T", [P, DC, PAIR, patches])
        downT = sb("down_T", [P, DC, tokens])
        probs = sb("probs", [half_rows, T, tokens])
        pT = split("probs_T", [half_rows, T, wide])
        y = sb("y", [half_rows, T, dim])
        ysq = sb("y_squared", [half_rows, T, dim])
        h2_both = sb("h_mid", [P, 2, T, dim])
        h2 = [h2_both[0:half_rows, i] for i in range(2)]
        z = sb("z_norm", [half_rows, T, dim])
        zT = split("z_T", [P, DC, wide])
        th = [sb(f"tanh{i}", [P, tokens]) for i in range(2)]
        ga = [sb(f"gated{i}", [P, tokens]) for i in range(2)]
        hid = [sb(f"hid{i}", [P, tokens]) for i in range(HIDS)]
        hidT = split("hid_T", [P, HC, wide])
        res_both = sb("result", [P, 2, T, dim])
        res = [res_both[0:half_rows, i] for i in range(2)]
        assert 2 * T * dim == DC * hidden
        wstage = [h2_both[:].rearrange("p a t d -> p (a t d)"), sb("w_stage", [P, DC * hidden])]
        wint = res_both[:].rearrange("p a t d -> p (a t d)").bitcast(I32)
        stats = [sb(f"bn{i}", [half_rows, T, 6]) for i in range(2)]
        mv = [sb(f"mean_var{i}", [half_rows, T, 2]) for i in range(2)]
        var_eps = [sb(f"var_eps{i}", [half_rows, T]) for i in range(2)]
        rstd = [sb(f"rstd{i}", [half_rows, T]) for i in range(2)]
        nmax = sb("minus_max", [half_rows, T])
        den = sb("denominator", [half_rows, T])
        rden = sb("one_over_denominator", [half_rows, T])
        neg_mean = sb("minus_mean", [half_rows, T])
        shift = sb("minus_mean_rstd", [half_rows, T])
        neg_one = sb("minus_one", [P, T])
        ssq = sb("y_square_sum", [half_rows, T])
        lo_max = sb("w_lo_max", [P, T])
        lo_any = sb("w_lo_any", [P, 2])
        lo_flag = sb("w_lo_flag", [1, 1], I32)
        rnorm = sb("one_over_norm", [half_rows, T])

        def psum(name):
            return ctx.enter_context(nc.psum_tensor(name, [P, 512], F32))

        tp = [psum(f"transposing{i}") for i in range(2)]
        ab = [psum(f"attention{i}") for i in range(3)]
        fb = [psum(f"feed_forward{i}") for i in range(3)]

        consts_set = sem("consts_set")
        ident_set = sem("ident_set")
        w_loaded = [sem(f"w_loaded{i}") for i in range(7)]
        pos_loaded = sem("pos_loaded")
        w_float = sem("w_float")
        we_hi = sem("we_hi")
        we_split = sem("we_split")
        pos_set = sem("pos_set")
        px_loaded = sem("px_loaded")
        px_moved = sem("px_moved")
        text_loaded = [sem(f"text_loaded{i}") for i in range(2)]
        stored = [sem(f"stored{i}") for i in range(2)]
        transposed = sem("transposed")
        tp_hi = sem("transposed_hi")
        tp_split = sem("transposed_split")
        embedded = sem("embedded")
        emb_out = sem("emb_out")
        bn_done = [sem(f"bn_done{i}") for i in range(2)]
        mv_done = [sem(f"mv_done{i}") for i in range(2)]
        eps_done = [sem(f"eps_done{i}") for i in range(2)]
        rstd_done = [sem(f"rstd_done{i}") for i in range(2)]
        normed = [sem(f"normed{i}") for i in range(2)]
        projected = sem("projected")
        proj_hi = sem("proj_hi")
        proj_split = sem("proj_split")
        negated = sem("negated")
        shifted = sem("shifted")
        x_hi = sem("x_hi")
        x_split = sem("x_split_done")
        weighted = sem("weighted")
        u_hi = sem("u_hi")
        u_split = sem("u_split")
        scored = sem("scored")
        maxed = sem("maxed")
        exped = sem("exped")
        rden_done = sem("rden_done")
        attended = sem("attended")
        y_done = sem("y_done")
        squared = sem("squared")
        rnorm_done = sem("rnorm_done")
        h2_done = sem("h2_done")
        gate_done = sem("gate_done")
        up_done = sem("up_done")
        tanh_done = sem("tanh_done")
        gated = sem("gated")
        hid_done = sem("hid_done")
        hid_hi = sem("hid_hi")
        hid_split = sem("hid_split")
        downed = sem("downed")
        down_out = sem("down_out")
        w_lo_seen = sem("w_lo_seen")
        dve_passed = sem("dve_passed")
        pool_passed = sem("pool_passed")

        def above_zero(count):
            return not isinstance(count, int) or count > 0

        def HID(m_par, c):
            return (m_par * HC + c) % HIDS

        FILL_NEEDS = [(1 if hi <= grid // 2 else 2) + 2 * half for half in range(2) for _, hi in FILL]

        def flat(pair_of_parts):
            return [t[:].rearrange("p a b -> p (a b)") for t in pair_of_parts]

        block = ctx.enter_context(nc.Block())

        @block.sync
        def _(sp):
            sp.dma_start(raw[:, :], x_rows[0:px_rows, :]).then_inc(px_loaded, 16)
            sp.dma_start(wstage[1][:, :].rearrange("p (c d) -> p c d", d=dim),
                         w_embed.rearrange("(c p) d -> p c d", p=P)).then_inc(w_loaded[3], 16)
            for par in range(2):
                sp.sem_inc(stored[par], STORES)
            sp.dma_start(wstage[0][:, 0:DC * dim].rearrange("p (c d) -> p c d", c=DC),
                         wq.rearrange("(c p) d -> p c d", p=P)).then_inc(w_loaded[0], 16)
            sp.dma_start(wstage[0][:, DC * dim:2 * DC * dim].rearrange("p (c d) -> p c d", c=DC),
                         wk.rearrange("(c p) d -> p c d", p=P)).then_inc(w_loaded[1], 16)
            sp.dma_start(wstage[0][:, 2 * DC * dim:3 * DC * dim].rearrange("p (c d) -> p c d", c=DC),
                         wv.rearrange("(c p) d -> p c d", p=P)).then_inc(w_loaded[2], 16)
            sp.dma_start(pos[:, :, :], pos_embed.rearrange("o (t p) d -> p (o t) d", p=half_rows)
                         ).then_inc(pos_loaded, 16)
            sp.dma_start(bias[:, :], b_embed.rearrange("(o d) -> o d", o=1).to_broadcast([half_rows, dim])
                         ).then_inc(pos_loaded, 16)
            sp.dma_start(h[0][0:text, 2, :], txt_rows[0:text, :]).then_inc(text_loaded[0], 16)
            sp.dma_start(wint[:, :].rearrange("p (c d) -> p c d", d=dim),
                         w_gate.rearrange("(c p) d -> p c d", p=P)).then_inc(w_loaded[4], 16)
            sp.wait_ge(px_moved, MOVES)
            sp.dma_start(raw[:, :], x_rows[px_rows:2 * px_rows, :]).then_inc(px_loaded, 16)
            sp.wait_ge(w_float, 1)
            sp.dma_start(wint[:, :].rearrange("p (c d) -> p c d", d=dim),
                         w_up.rearrange("(c p) d -> p c d", p=P)).then_inc(w_loaded[5], 16)
            sp.wait_ge(w_float, 2)
            sp.dma_start(wint[:, :].rearrange("p (c h) -> p c h", h=hidden),
                         w_down.rearrange("(c p) h -> p c h", p=P)).then_inc(w_loaded[6], 16)

            def store(m, par, results):
                sp.wait_ge(tp_split, results)
                sp.dma_start(out_rows[bass.ds(m * tokens, patches), :].rearrange("(t p) d -> p t d", p=half_rows),
                             res[par][:, 0:2, :]).then_inc(stored[par], 16)
                sp.dma_start(out_rows[bass.ds(m * tokens + patches, text), :],
                             res[par][0:text, 2, :]).then_inc(stored[par], 16)

            def slot(n, k, kind):
                at = Slot(kind, k)
                if kind in (SECOND, ODD):
                    sp.wait_ge(px_moved, MOVES * (k + 1))
                    sp.dma_start(raw[:, :], x_rows[bass.ds((k + 1) * px_rows, px_rows), :]
                                 ).then_inc(px_loaded, 16)
                par = 0 if kind in (SECOND, ODD, ODD_LAST, END) else 1
                if at.ahead:
                    if above_zero(3 * n):
                        sp.wait_ge(h2_done, 3 * n)
                    sp.dma_start(h[par][0:text, 2, :], txt_rows[bass.ds((n + 1) * text, text), :]
                                 ).then_inc(text_loaded[par], 16)
                if at.outs:
                    store(n - 2, 1 - par, at.use("out1") + 1)

            slot(0, 0, FIRST)
            slot(1, 1, SECOND)
            slot(2, 1, EVEN)
            with sp.Fori(2, pairs - 1) as k:
                slot(2 * k - 1, k, ODD)
                slot(2 * k, k, EVEN)
            slot(images - 3, pairs - 1, ODD_LAST)
            slot(images - 2, pairs - 1, EVEN_LAST)
            slot(images - 1, pairs, END)
            for par in range(2):
                store(images - 2 + par, par, Slot(END, pairs).end + 4 + 2 * par)
            for par in range(2):
                sp.wait_ge(stored[par], STORES * (pairs + 1))

        @block.gpsimd
        def _(pool):
            nc.gpsimd.memset(ident[:, :], 0.0).then_inc(ident_set, 1)
            pool.wait_ge(ident_set, 1)
            nc.gpsimd.affine_select(out=ident[:, :], in_=ident[:, :], compare_op=ALU.not_equal, fill=1.0,
                                    base=0, pattern=[[-1, P]], channel_multiplier=1).then_inc(ident_set, 1)
            nc.gpsimd.memset(eps[:, :], EPS)
            nc.gpsimd.memset(neg_half[:, :], -0.5)
            nc.gpsimd.memset(neg_one[:, :], -1.0)
            for t in (xT[0], xT[1], zT[0], zT[1], pT[0], pT[1], hidT[0], hidT[1]):
                nc.gpsimd.memset(t[:, :, tokens:wide].bitcast(F32), 0.0)
            for t in (den, ssq, mv[0], mv[1]):
                last_set = nc.gpsimd.memset(t[:], 1.0)
            last_set.then_inc(consts_set, 1)

            def inverse_std(which, n):
                pool.wait_ge(mv_done[which], 3 * n + 3)
                nc.gpsimd.tensor_tensor(var_eps[which][:, :], mv[which][:, :, 1], eps[0:half_rows, :],
                                        ALU.add).then_inc(eps_done[which], 1)
                pool.wait_ge(eps_done[which], n + 1)
                nc.gpsimd.tensor_tensor(rstd[which][:, :], var_eps[which][:, :], neg_half[0:half_rows, :],
                                        ALU.pow).then_inc(rstd_done[which], 1)

            def inverse_std_and_shift(n):
                pool.wait_ge(mv_done[0], 3 * n + 3)
                nc.gpsimd.tensor_tensor(neg_mean[:, :], mv[0][:, :, 0], neg_one[0:half_rows, :],
                                        ALU.mult).then_inc(negated, 1)
                inverse_std(0, n)
                pool.wait_ge(negated, n + 1)
                pool.wait_ge(rstd_done[0], n + 1)
                nc.gpsimd.tensor_tensor(shift[:, :], neg_mean[:, :], rstd[0][:, :], ALU.mult
                                        ).then_inc(shifted, 1)

            def normalise_x(n, par, t):
                if t == 0:
                    pool.wait_ge(shifted, n + 1)
                    pool.sem_inc(pool_passed, 1)
                r = ROWS[t]
                nc.gpsimd.tensor_scalar(xn[par][0:r, t, :], h[par][0:r, t, :], rstd[0][0:r, t:t + 1],
                                        shift[0:r, t:t + 1], ALU.mult, ALU.add).then_inc(normed[0], 1)

            def x_lo(n, par, t):
                r = ROWS[t]
                pool.wait_ge(x_hi, 3 * n + t + 1)
                nc.gpsimd.tensor_tensor(xs[1][0:r, t, :], xn[par][0:r, t, :], xs[0][0:r, t, :].bitcast(F32),
                                        ALU.subtract).then_inc(x_split, 1)

            def inverse_norm(n):
                pool.wait_ge(squared, 3 * n + 3)
                nc.gpsimd.tensor_tensor(rnorm[:, :], ssq[:, :], neg_half[0:half_rows, :],
                                        ALU.pow).then_inc(rnorm_done, 1)

            def hid_lo(m, m_par, c):
                pool.wait_ge(hid_hi, HC * m + c + 1)
                nc.gpsimd.tensor_tensor(hidT[1][:, c, 0:tokens], hid[HID(m_par, c)][:, :], hidT[0][:, c, 0:tokens].bitcast(F32),
                                        ALU.subtract).then_inc(hid_split, 1)

            inverse_std_and_shift(0)
            for t in range(T):
                normalise_x(0, 0, t)
            for t in range(T):
                x_lo(0, 0, t)

            def odd_slot(k, kind):
                n, at = 2 * k - 1, Slot(kind, k)
                m = n - 1
                if at.ff:
                    hid_lo(m, 0, 0)
                if at.ahead:
                    inverse_std_and_shift(n + 1)
                    for t in range(T):
                        normalise_x(n + 1, 0, t)
                if at.ff:
                    hid_lo(m, 0, 1)
                    hid_lo(m, 0, 2)
                inverse_norm(n)
                if at.ff:
                    hid_lo(m, 0, 3)
                    hid_lo(m, 0, 4)
                    hid_lo(m, 0, 5)
                inverse_std(1, n)
                if at.ahead:
                    for t in range(T):
                        x_lo(n + 1, 0, t)

            def even_slot(k, kind):
                n, at = 2 * k, Slot(kind, k)
                m = n - 1
                if at.ahead:
                    inverse_std_and_shift(n + 1)
                    normalise_x(n + 1, 1, 0)
                if at.ff:
                    hid_lo(m, 1, 0)
                if at.ahead:
                    normalise_x(n + 1, 1, 1)
                    normalise_x(n + 1, 1, 2)
                if at.ff:
                    hid_lo(m, 1, 1)
                    hid_lo(m, 1, 2)
                if kind == FIRST:
                    pool.wait_ge(w_lo_seen, 4)
                    nc.gpsimd.partition_all_reduce(lo_any[:, 1:2], lo_any[:, 0:1], P,
                                                   bass.bass_isa.ReduceOp.max).then_inc(w_lo_seen, 1)
                inverse_norm(n)
                if at.ff:
                    hid_lo(m, 1, 3)
                if at.ahead:
                    x_lo(n + 1, 1, 0)
                if at.ff:
                    hid_lo(m, 1, 4)
                    hid_lo(m, 1, 5)
                inverse_std(1, n)
                if at.ahead:
                    x_lo(n + 1, 1, 1)
                    x_lo(n + 1, 1, 2)

            even_slot(0, FIRST)
            odd_slot(1, SECOND)
            even_slot(1, EVEN)
            with pool.Fori(2, pairs - 1) as k:
                odd_slot(k, ODD)
                even_slot(k, EVEN)
            odd_slot(pairs - 1, ODD_LAST)
            even_slot(pairs - 1, EVEN_LAST)
            odd_slot(pairs, END)
            for c in range(HC):
                hid_lo(images - 1, 1, c)

        @block.tensor
        def _(pe):
            def mm3(dst, left, right, start, stop):
                nc.tensor.matmul(dst, left[0], right[0], start=start, stop=False)
                nc.tensor.matmul(dst, left[1], right[0], start=False, stop=False)
                return nc.tensor.matmul(dst, left[0], right[1], start=False, stop=stop)

            def transpose_group(use, blocks):
                pe.wait_ge(tp_split, use - 1)
                at = 0
                for src in blocks:
                    rows = src.shape[0]
                    done = nc.tensor.transpose(tp[use % 2][0:src.shape[1], at:at + rows], src,
                                               ident[0:rows, 0:rows])
                    at += rows
                done.then_inc(transposed, 1)

            def fill(j, pair, use, bank):
                pe.wait_ge(px_moved, MOVES * pair + FILL_NEEDS[j])
                lo, hi = FILL[j % 3]
                if above_zero(use - 1):
                    pe.wait_ge(tp_split, use - 1)
                for g in range(lo, hi):
                    src = pix[:, g, (j // 3) * HALF:(j // 3 + 1) * HALF]
                    done = nc.tensor.transpose(tp[bank][:, (g - lo) * px_rows:(g - lo + 1) * px_rows], src,
                                               ident[0:px_rows, 0:px_rows])
                done.then_inc(transposed, 1)

            def embed(f, patches_ready):
                if patches_ready is not None:
                    pe.wait_ge(tp_split, patches_ready)
                dst = ab[2][:, 0:PAIR * patches].rearrange("p (b s) -> p b s", b=PAIR)
                for c in range(channels):
                    for half in range(2):
                        done = mm3(dst, [w[:, 2 * c + half, f * P:(f + 1) * P] for w in we],
                                   [p[:, half, :].rearrange("p (b s) -> p b s", b=PAIR)
                                    [:, :, c * patches:(c + 1) * patches] for p in patT],
                                   c == 0 and half == 0, c == channels - 1 and half == 1)
                done.then_inc(embedded, 1)

            def transpose_embedding(par, outs, use, bank):
                pe.wait_ge(emb_out, outs)
                pe.wait_ge(tp_split, use - 1)
                for t in range(2):
                    for f in range(DC):
                        done = nc.tensor.transpose(tp[bank][0:half_rows, t * dim + f * P:t * dim + (f + 1) * P],
                                                   embT[:, f, par, t * half_rows:(t + 1) * half_rows], ident[:, :])
                done.then_inc(transposed, 1)

            def transpose_tokens(src, f, use, bank):
                pe.wait_ge(tp_split, use - 1)
                for t in range(T):
                    done = nc.tensor.transpose(tp[bank][:, TOKEN0[t]:TOKEN0[t] + ROWS[t]],
                                               src[0:ROWS[t], t, f * P:(f + 1) * P],
                                               ident[0:ROWS[t], 0:ROWS[t]])
                done.then_inc(transposed, 1)

            def transpose_x(n, par, f, use, bank):
                pe.wait_ge(normed[0], 3 * n + 3)
                transpose_tokens(xn[par], f, use, bank)

            def transpose_z(n, f, use, bank):
                pe.wait_ge(normed[1], 3 * n + 3)
                transpose_tokens(z, f, use, bank)

            def project(n, f, x_ready):
                pe.wait_ge(tp_split, x_ready)
                if above_zero(3 * n - 2 + f):
                    pe.wait_ge(y_done, 3 * n - 2 + f)
                for c in range(DC):
                    done = mm3(ab[f][:, 0:wide], [w[:, c, f * P:(f + 1) * P] for w in wqk],
                               [t[:, c, :] for t in xT], c == 0, c == DC - 1)
                done.then_inc(projected, 1)

            def scores(n, t):
                pe.wait_ge(proj_split, 2 * n + 2)
                if t == 2:
                    if above_zero(3 * n):
                        pe.wait_ge(y_done, 3 * n)
                for c in range(DC):
                    done = mm3(ab[t][0:ROWS[t], 0:wide], [q[:, c, TOKEN0[t]:TOKEN0[t] + ROWS[t]] for q in tT],
                               [q[:, c, :] for q in xT], c == 0, c == DC - 1)
                done.then_inc(scored, 1)

            def transpose_probs(n, j, use, bank):
                pe.wait_ge(tp_split, use - 1)
                for t in range(T):
                    if j == 0:
                        pe.wait_ge(exped, 3 * n + t + 1)
                    done = nc.tensor.transpose(tp[bank][0:ROWS[j], TOKEN0[t]:TOKEN0[t] + ROWS[t]],
                                               probs[0:ROWS[t], t, TOKEN0[j]:TOKEN0[j] + ROWS[j]],
                                               ident[0:ROWS[t], 0:ROWS[t]])
                done.then_inc(transposed, 1)

            def weigh(n, f, probs_ready):
                pe.wait_ge(tp_split, probs_ready)
                pe.wait_ge(x_split, 3 * n + 3)
                for j in range(T):
                    done = mm3(ab[f][:, 0:wide], [q[0:ROWS[j], j, f * P:(f + 1) * P] for q in xs],
                               [q[0:ROWS[j], j, :] for q in pT], j == 0, j == T - 1)
                done.then_inc(weighted, 1)

            def attend(n, t):
                pe.wait_ge(u_split, 2 * n + 2)
                for f in range(DC):
                    done = mm3(ab[t][0:ROWS[t], 0:dim], [q[:, f, TOKEN0[t]:TOKEN0[t] + ROWS[t]] for q in uT],
                               [w[:, f, :] for w in wvT], f == 0, f == DC - 1)
                done.then_inc(attended, 1)

            def mm_int(dst, weights, right, general, start, stop):
                if general:
                    return mm3(dst, weights, right, start, stop)
                nc.tensor.matmul(dst, weights[0], right[0], start=start, stop=False)
                return nc.tensor.matmul(dst, weights[0], right[1], start=False, stop=stop)

            def gate(m, c, general):
                bank = fb[(2 * c) % 3]
                if c == 0:
                    if above_zero(2 * m - 1):
                        pe.wait_ge(down_out, 2 * m - 1)
                elif c == 1:
                    if above_zero(HC * m):
                        pe.wait_ge(hid_done, HC * m)
                else:
                    pe.wait_ge(hid_done, HC * m + c - 1)
                for d in range(DC):
                    done = mm_int(bank[:, 0:wide], [w[:, d, c * P:(c + 1) * P] for w in wgT],
                                  [q[:, d, :] for q in zT], general, d == 0, d == DC - 1)
                done.then_inc(gate_done, 1)

            def up(m, c, general):
                bank = fb[(2 * c + 1) % 3]
                if c == 0:
                    if above_zero(2 * m):
                        pe.wait_ge(down_out, 2 * m)
                else:
                    pe.wait_ge(gated, HC * m + c)
                for d in range(DC):
                    done = mm_int(bank[:, 0:wide], [w[:, d, c * P:(c + 1) * P] for w in wuT],
                                  [q[:, d, :] for q in zT], general, d == 0, d == DC - 1)
                done.then_inc(up_done, 1)

            def down(m, f, general):
                if f == 0:
                    pe.wait_ge(hid_done, HC * m + HC - 1)
                else:
                    pe.wait_ge(gated, HC * m + HC)
                for c in range(HC):
                    if f == 0:
                        pe.wait_ge(hid_split, HC * m + c + 1)
                    done = mm_int(fb[f][:, 0:wide], [w[:, c, f * P:(f + 1) * P] for w in wdT],
                                  [q[:, c, :] for q in hidT], general, c == 0, c == HC - 1)
                done.then_inc(downed, 1)

            def transpose_down(m, i, use, bank):
                pe.wait_ge(tp_split, use - 1)
                for t in ((0, 1), (2,))[i]:
                    for f in range(DC):
                        if t == 0:
                            pe.wait_ge(down_out, 2 * m + f + 1)
                        at = t % 2 * dim + f * P
                        done = nc.tensor.transpose(tp[bank][0:ROWS[t], at:at + P],
                                                   downT[:, f, TOKEN0[t]:TOKEN0[t] + ROWS[t]], ident[:, :])
                done.then_inc(transposed, 1)

            pe.wait_ge(ident_set, 2)
            pe.wait_ge(consts_set, 1)
            for j in range(FILLS):
                fill(j, 0, j, j % 2)
            pe.wait_ge(we_split, 1)
            embed(0, FILLS)
            pe.wait_ge(w_loaded[0], 16)
            pe.wait_ge(w_loaded[1], 16)
            st = wstage[0]
            pe.wait_ge(tp_split, USE_WQK - 1)
            for d in range(DC):
                for e in range(DC):
                    done = nc.tensor.matmul(tp[USE_WQK % 2][:, d * dim:(d + 1) * dim],
                                            st[:, e * dim + d * P:e * dim + (d + 1) * P],
                                            st[:, (DC + e) * dim:(DC + e + 1) * dim],
                                            start=e == 0, stop=e == DC - 1)
            done.then_inc(transposed, 1)
            pe.wait_ge(w_loaded[2], 16)
            transpose_group(USE_WV, [st[:, (2 * DC + e) * dim + c * P:(2 * DC + e) * dim + (c + 1) * P]
                                     for c in range(DC) for e in range(DC)])
            pe.wait_ge(emb_out, 1)
            embed(1, None)
            transpose_embedding(0, DC, USE_H, USE_H % 2)
            for j in range(HALF_FILLS):
                fill(j, 1, USE_FILLS + j, (USE_FILLS + j) % 2)

            def transpose_weights(which, use, rows, cols):
                pe.wait_ge(w_float, which + 1)
                blocks = [wstage[(which + 1) % 2][:, (r * cols + c) * P:(r * cols + c + 1) * P]
                          for c in range(cols) for r in range(rows)]
                for g in range(3):
                    transpose_group(use + g, blocks[4 * g:4 * g + 4])

            transpose_weights(0, USE_GATE, HC, DC)
            for f in range(DC):
                transpose_x(0, 0, f, USE_X + f, (USE_X + f) % 2)
            for f in range(DC):
                project(0, f, USE_X + DC)
            transpose_weights(1, USE_UP, HC, DC)
            transpose_weights(2, USE_DOWN, DC, HC)

            def odd_slot(k, kind, general):
                n, at = 2 * k - 1, Slot(kind, k)
                m = n - 1
                scores(n, 0)
                if at.ff:
                    transpose_z(m, 0, at.use("z0"), at.bank("z0"))
                    transpose_z(m, 1, at.use("z1"), at.bank("z1"))
                scores(n, 1)
                if at.ahead:
                    pe.wait_ge(emb_out, DC * k + 1)
                scores(n, 2)
                if at.ff:
                    pe.wait_ge(tp_split, at.use("z1") + 1)
                    gate(m, 0, general)
                    up(m, 0, general)
                    gate(m, 1, general)
                transpose_probs(n, 0, at.use("probs0"), at.bank("probs0"))
                transpose_probs(n, 1, at.use("probs1"), at.bank("probs1"))
                if at.ahead:
                    embed(1, None)
                transpose_probs(n, 2, at.use("probs2"), at.bank("probs2"))
                if at.ff:
                    up(m, 1, general)
                    gate(m, 2, general)
                if at.ahead:
                    transpose_embedding(0, DC * k + 2, at.use("h"), at.bank("h"))
                if at.ff:
                    up(m, 2, general)
                weigh(n, 0, at.use("probs2") + 1)
                weigh(n, 1, at.use("probs2") + 1)
                if at.ff:
                    gate(m, 3, general)
                if at.outs:
                    transpose_down(n - 2, 0, at.use("out0"), at.bank("out0"))
                    transpose_down(n - 2, 1, at.use("out1"), at.bank("out1"))
                if at.ff:
                    up(m, 3, general)
                attend(n, 0)
                if at.refill:
                    fill(0, k + 1, at.use("fill0"), at.bank("fill0"))
                attend(n, 1)
                if at.ff:
                    gate(m, 4, general)
                if at.ahead:
                    pe.wait_ge(emb_out, DC * (k + 1))
                attend(n, 2)
                if at.ahead:
                    transpose_x(n + 1, 0, 0, at.use("x0"), at.bank("x0"))
                    transpose_x(n + 1, 0, 1, at.use("x1"), at.bank("x1"))
                if at.ff:
                    up(m, 4, general)
                    gate(m, 5, general)
                    up(m, 5, general)
                if at.refill:
                    fill(1, k + 1, at.use("fill1"), at.bank("fill1"))
                if at.ahead:
                    project(n + 1, 0, at.use("x1") + 1)
                    project(n + 1, 1, at.use("x1") + 1)
                if at.refill:
                    fill(2, k + 1, at.use("fill2"), at.bank("fill2"))
                if at.ff:
                    down(m, 0, general)
                    down(m, 1, general)

            def even_slot(k, kind, general):
                n, at = 2 * k, Slot(kind, k)
                m = n - 1
                scores(n, 0)
                scores(n, 1)
                if at.ff:
                    transpose_z(m, 0, at.use("z0"), at.bank("z0"))
                    transpose_z(m, 1, at.use("z1"), at.bank("z1"))
                scores(n, 2)
                if at.outs:
                    transpose_down(n - 2, 0, at.use("out0"), at.bank("out0"))
                if at.ahead:
                    transpose_embedding(1, DC * k + 2, at.use("h"), at.bank("h"))
                if at.ff:
                    pe.wait_ge(tp_split, at.use("z1") + 1)
                    gate(m, 0, general)
                    up(m, 0, general)
                transpose_probs(n, 0, at.use("probs0"), at.bank("probs0"))
                if at.ff:
                    gate(m, 1, general)
                transpose_probs(n, 1, at.use("probs1"), at.bank("probs1"))
                if at.ff:
                    up(m, 1, general)
                    gate(m, 2, general)
                transpose_probs(n, 2, at.use("probs2"), at.bank("probs2"))
                if at.ff:
                    up(m, 2, general)
                if at.refill:
                    fill(3, k + 1, at.use("fill3"), at.bank("fill3"))
                if at.ff:
                    gate(m, 3, general)
                if at.outs:
                    transpose_down(n - 2, 1, at.use("out1"), at.bank("out1"))
                weigh(n, 0, at.use("probs2") + 1)
                weigh(n, 1, at.use("probs2") + 1)
                if at.refill:
                    fill(4, k + 1, at.use("fill4"), at.bank("fill4"))
                if at.ff:
                    up(m, 3, general)
                    gate(m, 4, general)
                if at.refill:
                    fill(5, k + 1, at.use("fill5"), at.bank("fill5"))
                for t in range(T):
                    attend(n, t)
                if at.ff:
                    up(m, 4, general)
                if at.ahead:
                    transpose_x(n + 1, 1, 0, at.use("x0"), at.bank("x0"))
                if at.ff:
                    gate(m, 5, general)
                    up(m, 5, general)
                if at.ahead:
                    transpose_x(n + 1, 1, 1, at.use("x1"), at.bank("x1"))
                if at.refill:
                    pe.wait_ge(y_done, 3 * n + 3)
                    embed(0, at.use("fill5") + 1)
                if at.ahead:
                    project(n + 1, 0, at.use("x1") + 1)
                    project(n + 1, 1, at.use("x1") + 1)
                if at.ff:
                    down(m, 0, general)
                    down(m, 1, general)

            def pipeline(general):
                odd_slot(1, SECOND, general)
                even_slot(1, EVEN, general)
                with pe.Fori(2, pairs - 1) as k:
                    odd_slot(k, ODD, general)
                    even_slot(k, EVEN, general)
                odd_slot(pairs - 1, ODD_LAST, general)
                even_slot(pairs - 1, EVEN_LAST, general)
                odd_slot(pairs, END, general)
                end = Slot(END, pairs).end
                for f in range(DC):
                    transpose_z(images - 1, f, end + f, (end + f) % 2)
                for i in range(2):
                    transpose_down(images - 2, i, end + 2 + i, (end + i) % 2)
                pe.wait_ge(tp_split, end + 2)
                for c in range(HC):
                    gate(images - 1, c, general)
                    up(images - 1, c, general)
                for f in range(DC):
                    down(images - 1, f, general)
                for i in range(2):
                    transpose_down(images - 1, i, end + 4 + i, (end + i) % 2)

            even_slot(0, FIRST, False)
            pe.wait_ge(w_lo_seen, 6)
            general = pe.value_load(lo_flag[0:1, 0:1], min_val=0, max_val=1)
            with pe.If(general != 0):
                pipeline(True)
            with pe.Else():
                pipeline(False)

        @block.scalar
        def _(act):
            def hi_part(dst, src, after, count, signal):
                act.wait_ge(after, count)
                nc.scalar.activation(dst, src, ACT.Copy).then_inc(signal, 1)

            def fill_view(t, j):
                lo, hi = FILL[j % 3]
                return t[:, j // 3, :].rearrange("p (q g) -> p q g", g=grid)[:, :, lo:hi]

            def fill_bank(bank, j):
                lo, hi = FILL[j % 3]
                return tp[bank][:, 0:(hi - lo) * px_rows].rearrange("p (g q) -> p q g", q=px_rows)

            def fill_hi(j, use, bank):
                hi_part(fill_view(patT[0], j), fill_bank(bank, j), transposed, use + 1, tp_hi)

            def tokens_hi(dst, f, use, bank):
                hi_part(dst[:, f, 0:tokens], tp[bank][:, 0:tokens], transposed, use + 1, tp_hi)

            def move_pixels(pair, step):
                half, side_ = step // 2, step % 2
                cols = slice(side_ * grid // 2, (side_ + 1) * grid // 2)
                act.wait_ge(px_loaded, 16 * pair + 16)
                nc.scalar.activation(
                    pix[:, cols, half * HALF:(half + 1) * HALF].rearrange("r g (i j) -> r g i j", j=patch),
                    raw[:, :].rearrange("r (i g j) -> r g i j", i=patch, j=patch)
                    [:, cols, half * patch // 2:(half + 1) * patch // 2, :], ACT.Copy).then_inc(px_moved, 1)

            def embedding_out(f, pair):
                act.wait_ge(embedded, DC * pair + f + 1)
                nc.scalar.activation(embT[:, f, :, :],
                                     ab[2][:, 0:PAIR * patches].rearrange("p (b s) -> p b s", b=PAIR),
                                     ACT.Copy).then_inc(emb_out, 1)

            def exponentials(n, t):
                act.wait_ge(maxed, 3 * n + t + 1)
                nc.scalar.activation(probs[0:ROWS[t], t, :], ab[t][0:ROWS[t], 0:tokens], ACT.Exp,
                                     bias=nmax[0:ROWS[t], t:t + 1],
                                     accum_out=den[0:ROWS[t], t:t + 1]).then_inc(exped, 1)

            def probs_hi(j, use, bank):
                hi_part(pT[0][0:ROWS[j], j, 0:tokens], tp[bank][0:ROWS[j], 0:tokens], transposed, use + 1, tp_hi)

            def squares(n, t):
                act.wait_ge(y_done, 3 * n + t + 1)
                nc.scalar.activation(ysq[0:ROWS[t], t, :], y[0:ROWS[t], t, :], ACT.Square,
                                     accum_out=ssq[0:ROWS[t], t:t + 1]).then_inc(squared, 1)

            def x_part(n, par, t):
                if t == 0:
                    if above_zero(2 * n):
                        act.wait_ge(weighted, 2 * n)
                hi_part(xs[0][0:ROWS[t], t, :], xn[par][0:ROWS[t], t, :], normed[0], 3 * n + t + 1, x_hi)

            def projection_hi(n, f):
                hi_part(tT[0][:, f, :], ab[f][:, 0:tokens], projected, 2 * n + f + 1, proj_hi)

            def weighed_hi(n, f):
                hi_part(uT[0][:, f, :], ab[f][:, 0:tokens], weighted, 2 * n + f + 1, u_hi)

            def tanh(m, c):
                if above_zero(HC * m + c - 1):
                    act.wait_ge(gated, HC * m + c - 1)
                act.wait_ge(gate_done, HC * m + c + 1)
                nc.scalar.activation(th[c % 2][:, :], fb[(2 * c) % 3][:, 0:tokens], ACT.Tanh,
                                     scale=0.5 * INT_SCALE).then_inc(tanh_done, 1)

            def hidden_hi(m, m_par, c):
                hi_part(hidT[0][:, c, 0:tokens], hid[HID(m_par, c)][:, :], hid_done, HC * m + c + 1, hid_hi)

            def down_out_of_psum(m, f):
                act.wait_ge(downed, 2 * m + f + 1)
                nc.scalar.activation(downT[:, f, :], fb[f][:, 0:tokens], ACT.Copy).then_inc(down_out, 1)

            def weights_hi(dst, use):
                for g in range(3):
                    hi_part(flat(dst)[0][:, g * 512:(g + 1) * 512], tp[(use + g) % 2][:, :],
                            transposed, use + g + 1, tp_hi)

            for step in range(2):
                move_pixels(0, step)
            hi_part(flat(we)[0], wstage[1][:, :], w_loaded[3], 16, we_hi)
            for step in range(2, MOVES):
                move_pixels(0, step)
            for j in range(FILLS):
                fill_hi(j, j, j % 2)
            act.wait_ge(consts_set, 1)
            embedding_out(0, 0)
            for i, dst in enumerate((wqk, wvT)):
                hi_part(flat(dst)[0], tp[(USE_WQK + i) % 2][:, :], transposed, USE_WQK + i + 1, tp_hi)
            for step in range(2):
                move_pixels(1, step)
            embedding_out(1, 0)
            for j in range(HALF_FILLS):
                fill_hi(j, USE_FILLS + j, (USE_FILLS + j) % 2)
            weights_hi(wgT, USE_GATE)
            for f in range(DC):
                tokens_hi(xT[0], f, USE_X + f, (USE_X + f) % 2)
            for f in range(DC):
                projection_hi(0, f)
            for t in range(T):
                x_part(0, 0, t)
            weights_hi(wuT, USE_UP)
            weights_hi(wdT, USE_DOWN)

            def odd_slot(k, kind):
                n, at = 2 * k - 1, Slot(kind, k)
                m = n - 1
                if at.ff:
                    tokens_hi(zT[0], 0, at.use("z0"), at.bank("z0"))
                    tokens_hi(zT[0], 1, at.use("z1"), at.bank("z1"))
                for t in range(T):
                    exponentials(n, t)
                if at.ff:
                    tanh(m, 0)
                probs_hi(0, at.use("probs0"), at.bank("probs0"))
                probs_hi(1, at.use("probs1"), at.bank("probs1"))
                if at.ff:
                    tanh(m, 1)
                    hidden_hi(m, 0, 0)
                if at.ahead:
                    embedding_out(1, k)
                probs_hi(2, at.use("probs2"), at.bank("probs2"))
                if at.ff:
                    tanh(m, 2)
                    hidden_hi(m, 0, 1)
                if at.refill:
                    move_pixels(k + 1, 0)
                weighed_hi(n, 0)
                if at.refill:
                    move_pixels(k + 1, 1)
                weighed_hi(n, 1)
                if at.ff:
                    tanh(m, 3)
                    hidden_hi(m, 0, 2)
                if at.refill:
                    fill_hi(0, at.use("fill0"), at.bank("fill0"))
                squares(n, 0)
                if at.ff:
                    hidden_hi(m, 0, 3)
                squares(n, 1)
                if at.ff:
                    tanh(m, 4)
                if at.ahead:
                    tokens_hi(xT[0], 0, at.use("x0"), at.bank("x0"))
                squares(n, 2)
                if at.ahead:
                    tokens_hi(xT[0], 1, at.use("x1"), at.bank("x1"))
                if at.ff:
                    tanh(m, 5)
                    hidden_hi(m, 0, 4)
                    hidden_hi(m, 0, 5)
                if at.ahead:
                    x_part(n + 1, 0, 0)
                    projection_hi(n + 1, 0)
                    projection_hi(n + 1, 1)
                if at.refill:
                    fill_hi(1, at.use("fill1"), at.bank("fill1"))
                if at.ahead:
                    x_part(n + 1, 0, 1)
                    x_part(n + 1, 0, 2)
                if at.refill:
                    fill_hi(2, at.use("fill2"), at.bank("fill2"))
                if at.ff:
                    down_out_of_psum(m, 0)
                    down_out_of_psum(m, 1)

            def even_slot(k, kind):
                n, at = 2 * k, Slot(kind, k)
                m = n - 1
                if at.refill:
                    move_pixels(k + 1, 2)
                if at.ff:
                    tokens_hi(zT[0], 0, at.use("z0"), at.bank("z0"))
                    tokens_hi(zT[0], 1, at.use("z1"), at.bank("z1"))
                for t in range(T):
                    exponentials(n, t)
                if at.ff:
                    tanh(m, 0)
                probs_hi(0, at.use("probs0"), at.bank("probs0"))
                if at.ff:
                    tanh(m, 1)
                probs_hi(1, at.use("probs1"), at.bank("probs1"))
                if at.ff:
                    hidden_hi(m, 1, 0)
                probs_hi(2, at.use("probs2"), at.bank("probs2"))
                if at.ff:
                    tanh(m, 2)
                if at.refill:
                    move_pixels(k + 1, 3)
                    fill_hi(3, at.use("fill3"), at.bank("fill3"))
                weighed_hi(n, 0)
                if at.ff:
                    hidden_hi(m, 1, 1)
                    tanh(m, 3)
                weighed_hi(n, 1)
                if at.refill:
                    fill_hi(4, at.use("fill4"), at.bank("fill4"))
                if at.ff:
                    tanh(m, 4)
                    hidden_hi(m, 1, 2)
                if at.ahead:
                    x_part(n + 1, 1, 0)
                if at.ff:
                    hidden_hi(m, 1, 3)
                if at.refill:
                    fill_hi(5, at.use("fill5"), at.bank("fill5"))
                for t in range(T):
                    squares(n, t)
                if at.ff:
                    tanh(m, 5)
                if at.ahead:
                    tokens_hi(xT[0], 0, at.use("x0"), at.bank("x0"))
                    x_part(n + 1, 1, 1)
                    x_part(n + 1, 1, 2)
                    tokens_hi(xT[0], 1, at.use("x1"), at.bank("x1"))
                if at.ff:
                    hidden_hi(m, 1, 4)
                    hidden_hi(m, 1, 5)
                if at.refill:
                    embedding_out(0, k + 1)
                if at.ahead:
                    projection_hi(n + 1, 0)
                    projection_hi(n + 1, 1)
                if at.ff:
                    down_out_of_psum(m, 0)
                    down_out_of_psum(m, 1)

            even_slot(0, FIRST)
            odd_slot(1, SECOND)
            even_slot(1, EVEN)
            with act.Fori(2, pairs - 1) as k:
                odd_slot(k, ODD)
                even_slot(k, EVEN)
            odd_slot(pairs - 1, ODD_LAST)
            even_slot(pairs - 1, EVEN_LAST)
            odd_slot(pairs, END)
            end = Slot(END, pairs).end
            for f in range(DC):
                tokens_hi(zT[0], f, end + f, (end + f) % 2)
            for c in range(HC):
                tanh(images - 1, c)
                hidden_hi(images - 1, 1, c)
            for f in range(DC):
                down_out_of_psum(images - 1, f)

        @block.vector
        def _(dve):
            def lo_part(dst, src, hi, after, count, signal):
                dve.wait_ge(after, count)
                nc.vector.tensor_tensor(dst, src, hi.bitcast(F32), ALU.subtract).then_inc(signal, 1)

            def fill_lo(j, his, bank):
                lo, hi = FILL[j % 3]
                views = [t[:, j // 3, :].rearrange("p (q g) -> p q g", g=grid)[:, :, lo:hi] for t in patT]
                src = tp[bank][:, 0:(hi - lo) * px_rows].rearrange("p (g q) -> p q g", q=px_rows)
                lo_part(views[1], src, views[0], tp_hi, his, tp_split)

            def tokens_lo(dst, f, his, bank):
                lo_part(dst[1][:, f, 0:tokens], tp[bank][:, 0:tokens], dst[0][:, f, 0:tokens], tp_hi, his, tp_split)

            def projection_lo(n, f):
                lo_part(tT[1][:, f, :], ab[f][:, 0:tokens], tT[0][:, f, :], proj_hi, 2 * n + f + 1, proj_split)

            def weighed_lo(n, f):
                lo_part(uT[1][:, f, :], ab[f][:, 0:tokens], uT[0][:, f, :], u_hi, 2 * n + f + 1, u_split)

            def maxima(n, t):
                r = ROWS[t]
                dve.wait_ge(scored, 3 * n + t + 1)
                nc.vector.tensor_reduce(nmax[0:r, t:t + 1], ab[t][0:r, 0:tokens], AX_X, ALU.max,
                                        negate=True).then_inc(maxed, 1)

            def probs_lo(j, his, bank):
                r = ROWS[j]
                lo_part(pT[1][0:r, j, 0:tokens], tp[bank][0:r, 0:tokens], pT[0][0:r, j, 0:tokens], tp_hi, his, tp_split)

            def reciprocals(n):
                dve.wait_ge(exped, 3 * n + 3)
                nc.vector.reciprocal(rden[:, :], den[:, :]).then_inc(rden_done, 1)

            def add_attended(n, par, t):
                r = ROWS[t]
                if t == 0:
                    dve.wait_ge(rden_done, n + 1)
                dve.wait_ge(attended, 3 * n + t + 1)
                nc.vector.scalar_tensor_tensor(y[0:r, t, :], ab[t][0:r, 0:dim], rden[0:r, t:t + 1],
                                               xn[par][0:r, t, :], ALU.mult, ALU.add).then_inc(y_done, 1)

            def add_normed(n, par, t):
                r = ROWS[t]
                if t == 0:
                    dve.wait_ge(rnorm_done, n + 1)
                nc.vector.scalar_tensor_tensor(h2[par][0:r, t, :], y[0:r, t, :], rnorm[0:r, t:t + 1],
                                               h[par][0:r, t, :], ALU.mult, ALU.add).then_inc(h2_done, 1)

            def statistics(which, src, n, after, counts):
                for t in range(T):
                    dve.wait_ge(after[t], counts[t])
                    nc.vector.bn_stats(stats[which][0:ROWS[t], t, :], src[0:ROWS[t], t, :]
                                       ).then_inc(bn_done[which], 1)
                for t in range(T):
                    dve.wait_ge(bn_done[which], 3 * n + t + 1)
                    dve.sem_inc(dve_passed, 1)
                    nc.vector.bn_aggr(mv[which][0:ROWS[t], t, :], stats[which][0:ROWS[t], t, :]
                                      ).then_inc(mv_done[which], 1)

            def normalise_z(n, par, t):
                r = ROWS[t]
                if t == 0:
                    dve.wait_ge(rstd_done[1], n + 1)
                nc.vector.tensor_scalar(z[0:r, t, :], h2[par][0:r, t, :], mv[1][0:r, t, 0:1],
                                        rstd[1][0:r, t:t + 1], ALU.subtract, ALU.mult).then_inc(normed[1], 1)

            def add_positions(par, use, bank):
                dve.wait_ge(transposed, use + 1)
                nc.vector.tensor_tensor(h[par][:, 0:2, :], tp[bank][0:half_rows, :].rearrange("p (t d) -> p t d", t=2),
                                        pos[:, :, :], ALU.add).then_inc(tp_split, 1)

            def h_statistics(n, par, text_count, use):
                statistics(0, h[par], n, (tp_split, tp_split, text_loaded[par]), (use + 1, use + 1, text_count))

            def gate(m, c):
                dve.wait_ge(tanh_done, HC * m + c + 1)
                nc.vector.scalar_tensor_tensor(ga[c % 2][:, :], th[c % 2][:, :], 1.0,
                                               fb[(2 * c) % 3][:, 0:tokens], ALU.add, ALU.mult
                                               ).then_inc(gated, 1)

            def times_up(m, m_par, c):
                dve.wait_ge(gated, HC * m + c + 1)
                if above_zero(HC * m + c + 1 - HIDS):
                    dve.wait_ge(hid_split, HC * m + c + 1 - HIDS)
                dve.wait_ge(up_done, HC * m + c + 1)
                nc.vector.tensor_tensor(hid[HID(m_par, c)][:, :], ga[c % 2][:, :], fb[(2 * c + 1) % 3][:, 0:tokens],
                                        ALU.mult).then_inc(hid_done, 1)

            def finish(m, par, i, stores, use, bank):
                t0, t1 = ((0, 2), (2, 3))[i]
                r = ROWS[t0]
                dve.wait_ge(stored[par], stores)
                dve.wait_ge(transposed, use + 1)
                nc.vector.scalar_tensor_tensor(
                    res[par][0:r, t0:t1, :].rearrange("p t d -> p (t d)"), tp[bank][0:r, 0:(t1 - t0) * dim],
                    0.5 * INT_SCALE ** 3, h2[par][0:r, t0:t1, :].rearrange("p t d -> p (t d)"),
                    ALU.mult, ALU.add).then_inc(tp_split, 1)

            def weights_lo(dst, use):
                for g in range(3):
                    lo_part(flat(dst)[1][:, g * 512:(g + 1) * 512], tp[(use + g) % 2][:, :],
                            flat(dst)[0][:, g * 512:(g + 1) * 512], tp_hi, use + g, tp_split)

            def largest_lo(i, w, splits):
                dve.wait_ge(tp_split, splits)
                nc.vector.tensor_reduce(lo_max[:, i:i + 1], flat(w)[1].bitcast(F32), AX_X, ALU.max,
                                        apply_absolute_value=True).then_inc(w_lo_seen, 1)

            fill_lo(0, 1, 0)
            lo_part(flat(we)[1], wstage[1][:, :], flat(we)[0], we_hi, 1, we_split)
            for j in range(1, FILLS):
                fill_lo(j, j + 1, j % 2)
            dve.wait_ge(we_split, 1)
            dve.wait_ge(w_loaded[4], 16)
            nc.vector.tensor_copy(wstage[1][:, :], wint[:, :]).then_inc(w_float, 1)
            dve.wait_ge(pos_loaded, 32)
            for t in range(2):
                nc.vector.tensor_tensor(pos[:, t, :], pos[:, t, :], bias[:, :], ALU.add).then_inc(pos_set, 1)
            for i, dst in enumerate((wqk, wvT)):
                lo_part(flat(dst)[1], tp[(USE_WQK + i) % 2][:, :], flat(dst)[0], tp_hi, USE_WQK + i + 1, tp_split)
            dve.wait_ge(w_loaded[5], 16)
            nc.vector.tensor_copy(wstage[0][:, :], wint[:, :]).then_inc(w_float, 1)
            dve.wait_ge(pos_set, 2)
            dve.wait_ge(consts_set, 1)
            add_positions(0, USE_H, USE_H % 2)
            h_statistics(0, 0, TEXT_LOADED, USE_H)
            for j in range(HALF_FILLS):
                fill_lo(j, USE_FILLS + j, (USE_FILLS + j) % 2)
            weights_lo(wgT, USE_GATE)
            dve.wait_ge(w_loaded[6], 16)
            nc.vector.tensor_copy(wstage[1][:, :], wint[:, :]).then_inc(w_float, 1)
            for f in range(DC):
                tokens_lo(xT, f, USE_X + f, (USE_X + f) % 2)
            for f in range(DC):
                projection_lo(0, f)
            weights_lo(wuT, USE_UP)
            weights_lo(wdT, USE_DOWN)

            def odd_slot(k, kind):
                n, at = 2 * k - 1, Slot(kind, k)
                m = n - 1
                maxima(n, 0)
                if at.ff:
                    tokens_lo(zT, 0, at.his("z0"), at.bank("z0"))
                    tokens_lo(zT, 1, at.his("z1"), at.bank("z1"))
                maxima(n, 1)
                maxima(n, 2)
                reciprocals(n)
                if at.ff:
                    gate(m, 0)
                    times_up(m, 0, 0)
                probs_lo(0, at.his("probs0"), at.bank("probs0"))
                if at.ff:
                    gate(m, 1)
                probs_lo(1, at.his("probs1"), at.bank("probs1"))
                if at.ff:
                    times_up(m, 0, 1)
                probs_lo(2, at.his("probs2"), at.bank("probs2"))
                if at.ahead:
                    add_positions(0, at.use("h"), at.bank("h"))
                    h_statistics(n + 1, 0, TEXT_LOADED * (k + 1), at.use("h"))
                if at.ff:
                    gate(m, 2)
                weighed_lo(n, 0)
                if at.ff:
                    times_up(m, 0, 2)
                weighed_lo(n, 1)
                if at.outs:
                    finish(n - 2, 1, 0, STORES * (k - 1), at.use("out0"), at.bank("out0"))
                    finish(n - 2, 1, 1, STORES * (k - 1), at.use("out1"), at.bank("out1"))
                if at.ff:
                    gate(m, 3)
                add_attended(n, 1, 0)
                if at.ff:
                    times_up(m, 0, 3)
                add_attended(n, 1, 1)
                if at.refill:
                    fill_lo(0, at.his("fill0"), at.bank("fill0"))
                add_attended(n, 1, 2)
                if at.ff:
                    gate(m, 4)
                if at.ahead:
                    tokens_lo(xT, 0, at.his("x0"), at.bank("x0"))
                if at.ff:
                    times_up(m, 0, 4)
                if at.ahead:
                    tokens_lo(xT, 1, at.his("x1"), at.bank("x1"))
                if at.ff:
                    gate(m, 5)
                add_normed(n, 1, 0)
                if at.ff:
                    times_up(m, 0, 5)
                add_normed(n, 1, 1)
                add_normed(n, 1, 2)
                statistics(1, h2[1], n, (h2_done,) * 3, [3 * n + t + 1 for t in range(T)])
                if at.ahead:
                    projection_lo(n + 1, 0)
                if at.refill:
                    fill_lo(1, at.his("fill1"), at.bank("fill1"))
                if at.ahead:
                    projection_lo(n + 1, 1)
                for t in range(T):
                    normalise_z(n, 1, t)
                if at.refill:
                    fill_lo(2, at.his("fill2"), at.bank("fill2"))

            def even_slot(k, kind):
                n, at = 2 * k, Slot(kind, k)
                m = n - 1
                maxima(n, 0)
                maxima(n, 1)
                if at.ff:
                    tokens_lo(zT, 0, at.his("z0"), at.bank("z0"))
                    tokens_lo(zT, 1, at.his("z1"), at.bank("z1"))
                maxima(n, 2)
                if kind == FIRST:
                    largest_lo(0, wgT, USE_GATE + 3)
                if at.outs:
                    finish(n - 2, 0, 0, STORES * k, at.use("out0"), at.bank("out0"))
                if at.ahead:
                    add_positions(1, at.use("h"), at.bank("h"))
                if at.ff:
                    gate(m, 0)
                    times_up(m, 1, 0)
                probs_lo(0, at.his("probs0"), at.bank("probs0"))
                if at.ff:
                    gate(m, 1)
                probs_lo(1, at.his("probs1"), at.bank("probs1"))
                reciprocals(n)
                if at.ff:
                    times_up(m, 1, 1)
                probs_lo(2, at.his("probs2"), at.bank("probs2"))
                if kind == FIRST:
                    largest_lo(1, wuT, USE_UP + 3)
                if at.ahead:
                    h_statistics(n + 1, 1, TEXT_LOADED * (k + 1), at.use("h"))
                if at.ff:
                    gate(m, 2)
                if at.refill:
                    fill_lo(3, at.his("fill3"), at.bank("fill3"))
                if at.ff:
                    times_up(m, 1, 2)
                if at.outs:
                    finish(n - 2, 0, 1, STORES * k, at.use("out1"), at.bank("out1"))
                weighed_lo(n, 0)
                if at.ff:
                    gate(m, 3)
                weighed_lo(n, 1)
                if kind == FIRST:
                    largest_lo(2, wdT, USE_DOWN + 3)
                    dve.wait_ge(w_lo_seen, 3)
                    nc.vector.tensor_reduce(lo_any[:, 0:1], lo_max[:, :], AX_X, ALU.max).then_inc(w_lo_seen, 1)
                if at.ff:
                    times_up(m, 1, 3)
                if at.refill:
                    fill_lo(4, at.his("fill4"), at.bank("fill4"))
                if at.ff:
                    gate(m, 4)
                for t in range(T):
                    add_attended(n, 0, t)
                if at.refill:
                    fill_lo(5, at.his("fill5"), at.bank("fill5"))
                if at.ff:
                    times_up(m, 1, 4)
                    gate(m, 5)
                if at.ahead:
                    tokens_lo(xT, 0, at.his("x0"), at.bank("x0"))
                add_normed(n, 0, 0)
                if at.ff:
                    times_up(m, 1, 5)
                add_normed(n, 0, 1)
                if at.ahead:
                    tokens_lo(xT, 1, at.his("x1"), at.bank("x1"))
                add_normed(n, 0, 2)
                statistics(1, h2[0], n, (h2_done,) * 3, [3 * n + t + 1 for t in range(T)])
                if at.ahead:
                    projection_lo(n + 1, 0)
                    projection_lo(n + 1, 1)
                for t in range(T):
                    normalise_z(n, 0, t)

            even_slot(0, FIRST)
            dve.wait_ge(w_lo_seen, 5)
            nc.vector.tensor_scalar(lo_flag[0:1, 0:1], lo_any[0:1, 1:2], 0.0, None, ALU.is_gt
                                    ).then_inc(w_lo_seen, 1)
            odd_slot(1, SECOND)
            even_slot(1, EVEN)
            with dve.Fori(2, pairs - 1) as k:
                odd_slot(k, ODD)
                even_slot(k, EVEN)
            odd_slot(pairs - 1, ODD_LAST)
            even_slot(pairs - 1, EVEN_LAST)
            odd_slot(pairs, END)
            end, his = Slot(END, pairs).end, Slot(END, pairs).hi_end
            for f in range(DC):
                tokens_lo(zT, f, his + f + 1, (end + f) % 2)
            for i in range(2):
                finish(images - 2, 0, i, STORES * pairs, end + 2 + i, (end + i) % 2)
            for c in range(HC):
                gate(images - 1, c)
                times_up(images - 1, 1, c)
            for i in range(2):
                finish(images - 1, 1, i, STORES * pairs, end + 4 + i, (end + i) % 2)


_INS = ["x", "txt", "L0_tok_W_embed", "L0_tok_b_embed", "L0_tok_pos_embed", "L0_attn_Wq", "L0_attn_Wk",
        "L0_attn_Wv", "L0_ffn_w_gate", "L0_ffn_w_up", "L0_ffn_w_down"]


def kernel(**inputs):
    import numpy as np
    import concourse.bacc as bacc
    from concourse.bass_utils import run_bass_kernel_spmd

    nc = bacc.Bacc("TRN2", target_bir_lowering=False, num_devices=1)
    arrays, args = {}, []
    for name in _INS:
        a = np.ascontiguousarray(inputs[name])
        arrays[f"in_{name}"] = a
        args.append(nc.dram_tensor(f"in_{name}", a.shape, mybir.dt.from_np(a.dtype), kind="ExternalInput").ap())
    images, _, _, _ = inputs["x"].shape
    tokens = inputs["txt"].shape[1] + inputs["L0_tok_pos_embed"].shape[1]
    dim = inputs["txt"].shape[2]
    args.append(nc.dram_tensor("out_h", (images, tokens, dim), F32, kind="ExternalOutput").ap())
    fusion_layer(nc, *args)
    r = run_bass_kernel_spmd(nc, [arrays], core_ids=[0])
    return r.results[0]["out_h"]
```
